# Optimizing a Trainium2 kernel written in Bass

```python
import numpy as np
import jax
import jax.numpy as jnp

def _softmax(x, axis=-1):
    return jax.nn.softmax(x, axis=axis)

def _gelu(x):
    return jax.nn.gelu(x, approximate=True)

def _silu(x):
    return jax.nn.silu(x)

def _sigmoid(x):
    return jax.nn.sigmoid(x)

def _layernorm(x, axis=-1, eps=1e-05):
    m = jnp.mean(x, axis=axis, keepdims=True)
    v = jnp.var(x, axis=axis, keepdims=True)
    return (x - m) / jnp.sqrt(v + eps)

def _scatter_add(tgt, idx, src, axis=0):
    return tgt.at[idx].add(src)

def _segment_sum(src, seg, n):
    return jax.ops.segment_sum(src, seg, n)
kernel_name = 'mk_adj_ffn_d1_adj_r2_4be098'

def setup_inputs(seed: int=0):
    np.random.seed(seed)
    _w = jnp.asarray

    def _rec_inputs():
        import jax
        import jax.numpy as jnp
        _gk = jax.random.key(seed)
        x = -0.0002928 + 1 * jax.random.normal(jax.random.fold_in(_gk, 1), (8, 1024, 128), jnp.float32)
        _a = jax.random.bernoulli(jax.random.fold_in(_gk, 2), 0.0078125, (8, 1024, 1024))
        _af = _a.astype(jnp.float32)
        _af = _af * jax.random.uniform(jax.random.fold_in(_gk, 3), (8, 1024, 1024), jnp.float32, 0.05, 0.999995)
        adj = _af
        return (x, adj)
    x, adj = _rec_inputs()

    def _L0_gnn_setup():
        import jax, jax.numpy as jnp
        import numpy as np
        B, N, D = (4, 2048, 128)
        DENSITY = 0.02
        key = jax.random.key(seed)
        kx, ka1, ka2, kwt, kbt, kwh, kth = jax.random.split(key, 7)
        x = jax.random.normal(kx, (B, N, D), dtype=jnp.float32)
        mask = jax.random.uniform(ka1, (B, N, N)) < DENSITY
        vals = jax.random.uniform(ka2, (B, N, N), dtype=jnp.float32)
        adj = jnp.where(mask, vals, 0.0).astype(jnp.float32)
        s = 0.02
        W_t = s * jax.random.normal(kwt, (D, D), dtype=jnp.float32)
        b_t = s * jax.random.normal(kbt, (D,), dtype=jnp.float32)
        W_h = s * jax.random.normal(kwh, (D, D), dtype=jnp.float32)
        theta = s * jax.random.normal(kth, (D, D), dtype=jnp.float32)
        return {'x': x, 'adj': adj, 'W_t': W_t, 'b_t': b_t, 'W_h': W_h, 'theta': theta}
    _L0_gnn_all = _L0_gnn_setup()
    _L0_gnn_in = {k: v for k, v in _L0_gnn_all.items() if k in ('W_t', 'b_t', 'W_h', 'theta')}
    del _L0_gnn_all

    def _L0_ffn_setup():
        import jax, jax.numpy as jnp
        import numpy as np
        B, S, D, H, E, K = (8, 4096, 128, 512, 8, 2)
        key = jax.random.key(seed)
        ks = jax.random.split(key, 7)
        s_in = 1.0 / np.sqrt(D)
        s_hid = 1.0 / np.sqrt(H)
        return {'x': jax.random.normal(ks[0], (B, S, D), dtype=jnp.float32), 'Wg': jax.random.uniform(ks[1], (E, D), jnp.float32, -s_in, s_in), 'bg': jax.random.uniform(ks[2], (E,), jnp.float32, -s_in, s_in), 'W1': jax.random.uniform(ks[3], (E, H, D), jnp.float32, -s_in, s_in), 'b1': jax.random.uniform(ks[4], (E, H), jnp.float32, -s_in, s_in), 'W2': jax.random.uniform(ks[5], (E, D, H), jnp.float32, -s_hid, s_hid), 'b2': jax.random.uniform(ks[6], (E, D), jnp.float32, -s_hid, s_hid)}
    _L0_ffn_all = _L0_ffn_setup()
    _L0_ffn_in = {k: v for k, v in _L0_ffn_all.items() if k in ('Wg', 'bg', 'W1', 'b1', 'W2', 'b2')}
    del _L0_ffn_all
    return {'x': x, 'adj': adj, 'L0_gnn_W_t': _L0_gnn_in['W_t'], 'L0_gnn_b_t': _L0_gnn_in['b_t'], 'L0_gnn_W_h': _L0_gnn_in['W_h'], 'L0_gnn_theta': _L0_gnn_in['theta'], 'L0_ffn_Wg': _L0_ffn_in['Wg'], 'L0_ffn_bg': _L0_ffn_in['bg'], 'L0_ffn_W1': _L0_ffn_in['W1'], 'L0_ffn_b1': _L0_ffn_in['b1'], 'L0_ffn_W2': _L0_ffn_in['W2'], 'L0_ffn_b2': _L0_ffn_in['b2']}

def reference(x, adj, L0_gnn_W_t, L0_gnn_b_t, L0_gnn_W_h, L0_gnn_theta, L0_ffn_Wg, L0_ffn_bg, L0_ffn_W1, L0_ffn_b1, L0_ffn_W2, L0_ffn_b2):
    import jax
    import jax.numpy as jnp

    def _L0_gnn_ref(x, adj, W_t, b_t, W_h, theta):
        import jax, jax.numpy as jnp
        import numpy as np
        B, N, D = (4, 2048, 128)
        DENSITY = 0.02
        in_degrees = jnp.sum(adj, axis=-1)
        norm = jnp.power(in_degrees + 1e-06, -0.5)[..., None]
        f_hom = jnp.einsum('bnd,de->bne', x, theta) * norm
        f_hom = jnp.einsum('bnm,bmd->bnd', adj, f_hom) * norm
        f_het = jnp.einsum('bnd,de->bne', x, W_h)
        gate = jax.nn.sigmoid(jnp.einsum('bnd,de->bne', x, W_t) + b_t)
        out = gate * f_hom + (1.0 - gate) * f_het
        return jax.nn.elu(out)

    def _L0_ffn_ref(x, Wg, bg, W1, b1, W2, b2):
        import jax, jax.numpy as jnp
        import numpy as np
        B, S, D, H, E, K = (8, 4096, 128, 512, 8, 2)
        gate_scores = jnp.einsum('bsd,ed->bse', x, Wg) + bg
        topk_scores, topk_idx = jax.lax.top_k(gate_scores, K)
        topk_probs = jax.nn.softmax(topk_scores, axis=-1)
        combine = jnp.sum(topk_probs[..., None] * jax.nn.one_hot(topk_idx, E, dtype=x.dtype), axis=-2)
        out = jnp.zeros_like(x)
        for e in range(E):
            h = jax.nn.relu(jnp.einsum('bsd,hd->bsh', x, W1[e]) + b1[e])
            y = jnp.einsum('bsh,dh->bsd', h, W2[e]) + b2[e]
            out = out + combine[..., e:e + 1] * y
        return out
    x = x + _L0_gnn_ref(_layernorm(x, axis=-1), adj, L0_gnn_W_t, L0_gnn_b_t, L0_gnn_W_h, L0_gnn_theta)
    x = x + _L0_ffn_ref(_layernorm(x, axis=-1), L0_ffn_Wg, L0_ffn_bg, L0_ffn_W1, L0_ffn_b1, L0_ffn_W2, L0_ffn_b2)
    return x

_drawn_inputs = setup_inputs


def setup_inputs(seed=0):
    import zlib

    import numpy as np

    out = dict(_drawn_inputs(seed))
    spreads = {}
    factors = {'L0_gnn_W_t': 2.798, 'L0_gnn_b_t': 28.944, 'L0_ffn_b1': 3.88, 'L0_ffn_b2': 3.081}
    for name, (base, spread) in spreads.items():
        noise = np.random.default_rng([zlib.crc32(name.encode()), seed]).standard_normal(out[name].shape)
        drawn = base * np.exp(spread * noise) if base else spread * noise
        out[name] = jnp.asarray(drawn.astype(out[name].dtype))
    for name, factor in factors.items():
        out[name] = (out[name] * factor).astype(out[name].dtype)
    return out
```

```python
from contextlib import ExitStack

import concourse.bass as bass
from concourse import mybir

F32 = mybir.dt.float32
BF16 = mybir.dt.bfloat16
I32 = mybir.dt.int32
U32 = mybir.dt.uint32
ALU = mybir.AluOpType
ACT = mybir.ActivationFunctionType
AX_X = mybir.AxisListType.X

P = 128
EPS = 1e-5
DEG_EPS = 1e-6


def build(nc, x, adj_t, w_gnn, b_gate, wg_t, b_router, w1_t, w2_t, bias_e, out):
    B, _, TD = x.shape
    D = P
    T = TD // D
    N = P * T
    NE = wg_t.shape[1]
    H = w1_t.shape[1] // NE
    HC = H // P
    K = 2
    TOK = B * N
    REG = TOK + P
    FULL = K * TOK // P
    TILES = FULL + NE
    SPARE = TILES - FULL
    ROW = D + 2
    GN = 3 * D
    EB = H + D
    HALF = T // 2

    routed = nc.dram_tensor("routed", (NE * REG + SPARE * P, ROW), F32, kind="Internal").ap()
    expert_out = nc.dram_tensor("expert_out", (K * TOK + (NE + SPARE) * P, D), F32, kind="Internal").ap()
    expert_out_kb = expert_out[0:K * TOK, :].rearrange("(k b p t) d -> k b p (t d)", k=K, b=B, p=P)

    with ExitStack() as ctx:
        def sb(name, shape, dt=F32):
            return ctx.enter_context(nc.sbuf_tensor(name, shape, dt))

        def ps(name, shape):
            return ctx.enter_context(nc.psum_tensor(name, shape, F32))

        def sem(name):
            return ctx.enter_context(nc.semaphore(name))

        w_gnn_sb = sb("w_gnn_sb", [P, GN])
        wg_sb = sb("wg_sb", [P, NE])
        b_gate_sb = sb("b_gate_sb", [P, D])
        b_router_sb = sb("b_router_sb", [P, NE])
        w1_sb = sb("w1_sb", [P, NE * H])
        w2_sb = sb("w2_sb", [P, NE * H])
        ident = sb("ident", [P, P])
        ones_col = sb("ones_col", [P, 1])
        before = sb("before", [P, P], BF16)
        ones_bf = sb("ones_bf", [P, P], BF16)
        iota_e = sb("iota_e", [P, NE])
        minus_half = sb("minus_half", [P, T])

        adj_sb = sb("adj_sb", [P, 2, T * N])
        x1 = sb("x1", [P, B * TD])
        xn = sb("xn", [P, T, D])
        xn_t = sb("xn_t", [P, N])
        f_hom = sb("f_hom", [P, T, D])
        het_gate = sb("het_gate", [P, 2, T, 2 * D])
        col_sum_v = sb("col_sum_v", [P, N])
        col_sum_g = sb("col_sum_g", [P, N])
        x2n_t = sb("x2n_t", [P, N])
        z_sb = sb("z_sb", [P, T, D])
        neg_sb = sb("neg_sb", [P, T, D])
        stats = sb("stats", [P, 2, T, 6])
        mean_var = sb("mean_var", [P, 2, T, 2])
        rstd = sb("rstd", [P, 2, T])
        deg_sb = sb("deg_sb", [P, T])
        norm = sb("norm", [P, 2, T])
        payload = sb("payload", [P, 2, K, T, ROW])
        scores = sb("scores", [P, T, NE])
        top = sb("top", [P, T, 8])
        top_at = sb("top_at", [P, T, 8], U32)
        top_f = sb("top_f", [P, K, T])
        chosen = sb("chosen", [P, K, T, NE])
        picked = sb("picked", [P, T, NE], BF16)
        place = sb("place", [P, T, NE])
        place_k = sb("place_k", [P, K, T, NE])
        slot_f = sb("slot_f", [P, K, T])
        slot = sb("slot", [P, 2, K, T], I32)
        next_row = sb("next_row", [P, NE])
        p_exp = sb("p_exp", [P, T])
        p_sum = sb("p_sum", [P, T])

        used = [0, 0]

        def in_adj(buf, n):
            at = used[buf]
            used[buf] += n
            assert used[buf] <= T * N
            return adj_sb[:, buf, at:at + n]

        bias_sb = in_adj(0, NE * EB)
        pad_rows = in_adj(0, NE * ROW).rearrange("p (e r) -> p e r", r=ROW)
        spare_rows = in_adj(0, SPARE * ROW).rearrange("p (e r) -> p e r", r=ROW)
        pad_slot = in_adj(0, NE).bitcast(I32)
        tile_iota = in_adj(1, TILES)
        rt = in_adj(1, K * ROW * 2).rearrange("p (s r) -> p s r", r=ROW)
        rt_t = in_adj(1, 2 * P).rearrange("p (s n) -> p s n", s=2)
        h_sb = in_adj(1, 2 * H).rearrange("p (s n) -> p s n", s=2)
        h_t = in_adj(1, 2 * H).rearrange("p (s n) -> p s n", s=2)
        y_b = in_adj(1, 2 * D).rearrange("p (s n) -> p s n", s=2)
        y_out = in_adj(1, 4 * D).rearrange("p (s n) -> p s n", s=4)
        y_in = in_adj(1, 2 * K * TD).rearrange("p (s k n) -> p s k n", s=2, k=K)
        part_iota = sb("part_iota", [P, 1])
        count_i = sb("count_i", [P, NE], I32)
        tiles_e = sb("tiles_e", [P, NE])
        tiles_end = sb("tiles_end", [P, NE])
        skip_e = sb("skip_e", [P, NE])
        reach = sb("reach", [P, TILES])
        tile_e = sb("tile_e", [P, TILES])
        tile_row = sb("tile_row", [P, TILES])
        tab_w = sb("tab_w", [P, TILES], I32)
        tab_b = sb("tab_b", [P, TILES], I32)
        tab_row = sb("tab_row", [P, TILES], I32)

        bank = [ps(f"bank{i}", [P, 512]) for i in range(8)]
        hom_ps = bank[0:2]
        turn_ps = bank[2:4]
        proj_ps = bank[4:6]
        gate_ps, deg_ps = bank[6][:, 0:T * NE], bank[6][:, 128:128 + T]
        rank_ps, total_ps = bank[7][:, 0:T * NE], bank[7][:, 128:128 + NE]

        s_const = sem("s_const")
        s_wexp = sem("s_wexp")
        s_bias = sem("s_bias")
        x_loaded = [sem(f"x_loaded{i}") for i in range(2)]
        adj_loaded = [sem(f"adj_loaded{i}") for i in range(2)]
        iotas = sem("iotas")
        pool_const = sem("pool_const")
        dve_const = sem("dve_const")
        stats_ready = [sem(f"stats_ready{i}") for i in range(2)]
        rstd_ready = [sem(f"rstd_ready{i}") for i in range(2)]
        xn_ready = sem("xn_ready")
        turned1, turned2 = sem("turned1"), sem("turned2")
        xn_t_ready, x2n_t_ready = sem("xn_t_ready"), sem("x2n_t_ready")
        sum_v_ready, sum_g_ready = sem("sum_v_ready"), sem("sum_g_ready")
        deg_summed, deg_read, norm_ready = sem("deg_summed"), sem("deg_read"), sem("norm_ready")
        projected, proj_read = sem("projected"), sem("proj_read")
        gate_biased, gate_ready = sem("gate_biased"), sem("gate_ready")
        hom_ready, hom_read = sem("hom_ready"), sem("hom_read")
        z_ready, z_negated, exp_ready = sem("z_ready"), sem("z_negated"), sem("exp_ready")
        x2n_ready = sem("x2n_ready")
        gated, scores_ready, gaps_ready = sem("gated"), sem("scores_ready"), sem("gaps_ready")
        picked_ready, ranked, ranks_read = sem("picked_ready"), sem("ranked"), sem("ranks_read")
        p_exp_ready = sem("p_exp_ready")
        slots_ready, copied = sem("slots_ready"), sem("copied")
        scattered = [sem(f"scattered{i}") for i in range(2)]
        dve_chain, pool_chain, pool_waits = sem("dve_chain"), sem("pool_chain"), sem("pool_waits")
        spares_written = sem("spares_written")
        pads_ready, pads_written = sem("pads_ready"), sem("pads_written")
        pad_slots_ready, tables_ready = sem("pad_slots_ready"), sem("tables_ready")
        rt_loaded = [sem(f"rt_loaded{i}") for i in range(4)]
        rt_turned, rt_t_ready = sem("rt_turned"), sem("rt_t_ready")
        h_ready, h_biased = sem("h_ready"), sem("h_biased")
        h_turned, h_t_ready = sem("h_turned"), sem("h_t_ready")
        y_ready, y_biased, y_scaled = sem("y_ready"), sem("y_biased"), sem("y_scaled")
        returned = [sem(f"returned{i}") for i in range(4)]
        y_loaded = [sem(f"y_loaded{i}") for i in range(2)]
        out_ready = sem("out_ready")
        stored = sem("stored")

        block = ctx.enter_context(nc.Block())
        QTR = T * N // 4

        def cols(at, n):
            return bass.ds(at, n)

        @block.sync
        def _(sp):
            def load(b, par, r):
                if not isinstance(b, int) or b >= 2:
                    sp.wait_ge(hom_ready, 2 * (b - 1))
                sp.dma_start(x1[:, cols(b * TD, TD)], x[bass.ds(b, 1), :, :].rearrange("b p n -> (b p) n")
                             ).then_inc(x_loaded[par], 16)
                for q in range(4):
                    sp.dma_start(adj_sb[:, par, q * QTR:(q + 1) * QTR],
                                 adj_t[bass.ds(b, 1), :, q * QTR:(q + 1) * QTR].rearrange("b p n -> (b p) n")
                                 ).then_inc(adj_loaded[par], 16)

            load(0, 0, 0)
            for dst, src in ((w_gnn_sb, w_gnn), (b_gate_sb, b_gate), (wg_sb, wg_t), (b_router_sb, b_router)):
                sp.dma_start(dst[:, :], src).then_inc(s_const, 16)
            load(1, 1, 0)
            sp.dma_start(w1_sb[:, :], w1_t).then_inc(s_wexp, 16)
            sp.dma_start(w2_sb[:, :], w2_t).then_inc(s_wexp, 16)
            with sp.Fori(1, B // 2) as r:
                load(2 * r, 0, r)
                load(2 * r + 1, 1, r)
            sp.wait_ge(hom_ready, 2 * (B - 1))
            sp.dma_start(bias_sb, bias_e).then_inc(s_bias, 16)
            sp.wait_ge(pads_ready, 1)
            for j in range(SPARE):
                sp.dma_start(routed[NE * REG + j * P:NE * REG + (j + 1) * P, :], spare_rows[:, j, :]
                             ).then_inc(spares_written, 16)

            sp.wait_ge(tables_ready, 1)
            for par in range(2):
                sp.wait_ge(scattered[par], 16 * K * T * B // 2)
            sp.wait_ge(pads_written, 16 * NE)
            sp.wait_ge(spares_written, 16 * SPARE)

            def load_tile(t, s):
                row = sp.value_load(tab_row[0:1, cols(t, 1)], min_val=0, max_val=NE * REG + (SPARE - 1) * P)
                sp.dma_start(rt[:, s, :], routed[bass.ds(row, P), :]).then_inc(rt_loaded[s], 16)

            for t in range(4):
                load_tile(t, t)
            with sp.Fori(1, TILES // 4) as i:
                for s in range(4):
                    sp.wait_ge(returned[s], 16 * i)
                    load_tile(4 * i + s, s)
            for s in range(4):
                sp.wait_ge(returned[s], 16 * (TILES // 4))

            def load_y(b, par):
                for k in range(K):
                    sp.dma_start(y_in[:, par, k, :],
                                 expert_out_kb[k, bass.ds(b, 1), :, :].rearrange("b p n -> (b p) n")
                                 ).then_inc(y_loaded[par], 16)

            load_y(0, 0)
            load_y(1, 1)
            with sp.Fori(1, B // 2) as r:
                for par in range(2):
                    sp.wait_ge(out_ready, 2 * (r - 1) + par + 1)
                    load_y(2 * r + par, par)

        @block.gpsimd
        def _(pool):
            pool.memset(ident[:, :], 0.0).then_inc(pool_chain, 1)
            pool.memset(ones_bf[:, :], 1.0).then_inc(pool_chain, 1)
            pool.memset(ones_col[:, :], 1.0)
            pool.memset(minus_half[:, :], -0.5)
            pool.wait_ge(pool_chain, 2)
            pool.affine_select(out=ident[:, :], in_=ident[:, :], compare_op=ALU.not_equal, fill=1.0, base=0,
                               pattern=[[-1, P]], channel_multiplier=1)
            pool.affine_select(out=before[:, :], in_=ones_bf[:, :], compare_op=ALU.is_gt, fill=0.0, base=0,
                               pattern=[[1, P]], channel_multiplier=-1)
            pool.iota(iota_e[:, :], pattern=[[1, NE]], base=0, channel_multiplier=0,
                      allow_small_or_imprecise_dtypes=True)
            pool.iota(next_row[:, :], pattern=[[REG, NE]], base=0, channel_multiplier=0,
                      allow_small_or_imprecise_dtypes=True)
            pool.iota(part_iota[:, :], pattern=[[0, 1]], base=0, channel_multiplier=1,
                      allow_small_or_imprecise_dtypes=True)
            for par in range(2):
                dest = payload[:, par, :, :, D:D + 1].bitcast(I32)
                last = pool.iota(dest, pattern=[[TOK, K], [1, T], [0, 1]], base=(par - 2) * N,
                                 channel_multiplier=T)
            last.then_inc(pool_const, 1)

            def held():
                pool.sem_inc(pool_waits, 1)

            def rstd_of(ln, b):
                pool.sem_clear(pool_chain)
                pool.wait_ge(stats_ready[ln], b + 1)
                held()
                pool.tensor_scalar(rstd[:, ln, :], mean_var[:, ln, :, 1], EPS, None, ALU.add).then_inc(pool_chain, 1)
                pool.wait_ge(pool_chain, 1)
                pool.tensor_tensor(rstd[:, ln, :], rstd[:, ln, :], minus_half[:, :], ALU.pow
                                   ).then_inc(rstd_ready[ln], 1)

            def column_sums(b, par, r):
                pool.sem_clear(pool_chain)
                pool.wait_ge(adj_loaded[par], 64 * (r + 1))
                a = adj_sb[:, par, :].rearrange("p (c n) -> p c n", c=T)
                if not isinstance(b, int) or b >= 1:
                    pool.wait_ge(deg_summed, b)
                pool.tensor_tensor(col_sum_g[:, :], a[:, 5, :], a[:, 6, :], ALU.add).then_inc(pool_chain, 1)
                pool.wait_ge(pool_chain, 1)
                pool.tensor_tensor(col_sum_g[:, :], col_sum_g[:, :], a[:, 7, :], ALU.add).then_inc(sum_g_ready, 1)

            def degree_norm(b, par):
                pool.wait_ge(deg_read, b + 1)
                pool.tensor_tensor(norm[:, par, :], deg_sb[:, :], minus_half[:, :], ALU.pow).then_inc(norm_ready, 1)

            def gate_bias(b, par):
                pool.wait_ge(proj_read, T * (b + 1))
                g = het_gate[:, par, :, D:2 * D]
                pool.tensor_tensor(g, g, b_gate_sb[:, :].rearrange("p (o d) -> p o d", o=1).broadcast_to((P, T, D)),
                                   ALU.add).then_inc(gate_biased, 1)

            def copy_rows(b, par):
                pool.wait_ge(x2n_ready, b + 1)
                held()
                pool.tensor_copy(payload[:, par, 1, :, 0:D], payload[:, par, 0, :, 0:D]).then_inc(copied, 1)

            def scatter(b, par):
                pool.wait_ge(slots_ready, b + 1)
                pool.wait_ge(copied, b + 1)
                held()
                for k in range(K):
                    for t in range(T):
                        pool.indirect_dma_start(
                            routed[:, :], bass.IndirectOffsetOnAxis(ap=slot[:, par, k, t:t + 1], axis=0),
                            payload[:, par, k, t, :], None).then_inc(scattered[par], 16)

            def first_half(b, par, r):
                rstd_of(0, b)
                column_sums(b, par, r)
                degree_norm(b, par)
                gate_bias(b, par)

            def step(b, par, r, prev=True, nxt=True):
                if nxt:
                    rstd_of(0, b + 1)
                    column_sums(b + 1, 1 - par, r + par)
                if prev:
                    scatter(b - 1, 1 - par)
                if nxt:
                    degree_norm(b + 1, 1 - par)
                rstd_of(1, b)
                copy_rows(b, par)
                if nxt:
                    gate_bias(b + 1, 1 - par)

            pool.wait_ge(s_const, 64)
            first_half(0, 0, 0)
            step(0, 0, 0, prev=False)
            with pool.Fori(0, B // 2 - 1) as i:
                step(2 * i + 1, 1, i)
                step(2 * i + 2, 0, i + 1)
            step(B - 1, 1, B // 2 - 1, nxt=False)
            pool.wait_ge(hom_ready, 2 * B)
            pool.sem_clear(pool_chain)
            pool.memset(pad_rows, 0.0).then_inc(pool_chain, 1)
            pool.memset(spare_rows, 0.0).then_inc(pool_chain, 1)
            pool.wait_ge(pool_chain, 2)
            pool.iota(pad_rows[:, :, D:D + 1].bitcast(I32), pattern=[[P, NE], [0, 1]], base=K * TOK,
                      channel_multiplier=1)
            pool.iota(spare_rows[:, :, D:D + 1].bitcast(I32), pattern=[[P, SPARE], [0, 1]],
                      base=K * TOK + NE * P, channel_multiplier=1).then_inc(pads_ready, 1)
            pool.iota(tile_iota, pattern=[[1, TILES]], base=0, channel_multiplier=0,
                      allow_small_or_imprecise_dtypes=True).then_inc(iotas, 1)
            scatter(B - 1, 1)
            pool.wait_ge(pads_ready, 1)
            pool.wait_ge(pad_slots_ready, 1)
            for e in range(NE):
                pool.indirect_dma_start(
                    routed[:, :], bass.IndirectOffsetOnAxis(ap=pad_slot[:, e:e + 1], axis=0),
                    pad_rows[:, e, :], None).then_inc(pads_written, 16)

            def send(t, s):
                pool.wait_ge(y_scaled, t + 1)
                held()
                pool.indirect_dma_start(
                    expert_out[:, :], bass.IndirectOffsetOnAxis(ap=rt[:, s, D:D + 1].bitcast(I32), axis=0),
                    y_out[:, s, :], None).then_inc(returned[s], 16)

            with pool.Fori(0, TILES // 4) as i:
                for s in range(4):
                    send(4 * i + s, s)

        @block.tensor
        def _(pe):
            def turn_xn(b):
                pe.wait_ge(xn_ready, b + 1)
                for h in range(2):
                    if not isinstance(b, int) or b >= 2:
                        pe.wait_ge(x2n_t_ready, 2 * (b - 2) + h + 1)
                    for j in range(HALF):
                        m = pe.transpose(turn_ps[h][:, j * P:(j + 1) * P], xn[:, h * HALF + j, :], ident[:, :])
                    m.then_inc(turned1, 1)

            def turn_x2n(b, par, first=True):
                pe.wait_ge(x2n_ready, b + 1)
                for h in range(2):
                    pe.wait_ge(xn_t_ready, 2 * (b + (1 if first else 0)) + h + 1)
                    for j in range(HALF):
                        m = pe.transpose(turn_ps[h][:, j * P:(j + 1) * P],
                                         payload[:, par, 0, h * HALF + j, 0:D], ident[:, :])
                    m.then_inc(turned2, 1)

            def router(b):
                pe.wait_ge(x2n_t_ready, 2 * (b + 1))
                pe.wait_ge(deg_read, min(b + 2, B) if isinstance(b, int) else b + 2)
                for t in range(T):
                    m = pe.matmul(gate_ps[:, t * NE:(t + 1) * NE], x2n_t[:, t * P:(t + 1) * P], wg_sb[:, :],
                                  start=True, stop=True)
                m.then_inc(gated, 1)

            def ranks(b):
                pe.wait_ge(picked_ready, b + 1)
                flat = picked[:, :, :].rearrange("p t e -> p (t e)")
                pe.matmul(rank_ps, before[:, :], flat, start=True, stop=False, skip_group_check=True)
                for s in range(1, T):
                    pe.matmul(rank_ps[:, s * NE:], ones_bf[:, :], flat[:, 0:(T - s) * NE], start=False,
                              stop=(s == T - 1), skip_group_check=True)
                for t in range(T):
                    m = pe.matmul(total_ps, ones_bf[:, :], picked[:, t, :], start=(t == 0), stop=(t == T - 1),
                                  skip_group_check=True)
                m.then_inc(ranked, 1)

            def degree(b):
                pe.wait_ge(sum_v_ready, b + 1)
                pe.wait_ge(sum_g_ready, b + 1)
                if not isinstance(b, int) or b >= 2:
                    pe.wait_ge(scores_ready, b - 1)
                for t in range(T):
                    pe.matmul(deg_ps[:, t:t + 1], col_sum_v[:, t * P:(t + 1) * P], ones_col[:, :],
                              start=True, stop=False)
                    m = pe.matmul(deg_ps[:, t:t + 1], col_sum_g[:, t * P:(t + 1) * P], ones_col[:, :],
                                  start=False, stop=True)
                m.then_inc(deg_summed, 1)

            def project(b):
                for t in range(T):
                    if t % HALF == 0:
                        pe.wait_ge(xn_t_ready, 2 * b + t // HALF + 1)
                    if not isinstance(b, int) or b * T + t >= 2:
                        pe.wait_ge(proj_read, T * b + t - 1)
                    pe.matmul(proj_ps[t % 2][:, 0:GN], xn_t[:, t * P:(t + 1) * P], w_gnn_sb[:, :],
                              start=True, stop=True).then_inc(projected, 1)

            def aggregate(b, par, tiles, wait=False, done=False):
                h = tiles[0] // HALF
                if wait:
                    pe.wait_ge(proj_read, T * (b + 1))
                    if not isinstance(b, int) or b >= 1:
                        pe.wait_ge(hom_read, 2 * (b - 1) + h + 1)
                for t in tiles:
                    for c in range(T):
                        at = (c * T + t) * P
                        m = pe.matmul(hom_ps[h][:, (t % HALF) * P:(t % HALF + 1) * P], adj_sb[:, par, at:at + P],
                                      f_hom[:, c, :], start=(c == 0), stop=(c == T - 1))
                if done:
                    m.then_inc(hom_ready, 1)

            def step(b, par, prev=True, nxt=True):
                aggregate(b, par, range(0, HALF), wait=True, done=True)
                if prev:
                    turn_x2n(b - 1, 1 - par)
                    router(b - 1)
                if nxt:
                    turn_xn(b + 1)
                aggregate(b, par, range(HALF, T - 2), wait=True)
                if prev:
                    ranks(b - 1)
                aggregate(b, par, range(T - 2, T), done=True)
                if nxt:
                    degree(b + 1)
                    project(b + 1)

            pe.wait_ge(pool_const, 1)
            pe.wait_ge(s_const, 64)
            turn_xn(0)
            degree(0)
            project(0)
            step(0, 0, prev=False)
            with pe.Fori(0, B // 2 - 1) as i:
                step(2 * i + 1, 1)
                step(2 * i + 2, 0)
            step(B - 1, 1, nxt=False)
            turn_x2n(B - 1, 1, first=False)
            router(B - 1)
            ranks(B - 1)

            def tile_step(i, c):
                tau = 4 * i + c
                known = isinstance(tau, int)
                t = tau + 2
                if not known or t < TILES:
                    s = (c + 2) % 4
                    pe.wait_ge(rt_loaded[s], 16 * (i + (c + 2) // 4 + 1))
                    pe.transpose(bank[c % 2][:, 0:P], rt[:, s, 0:D], ident[:, :]).then_inc(rt_turned, 1)
                t = tau + 1
                if not known or 0 <= t < TILES:
                    col = pe.value_load(tab_w[0:1, cols(t, 1)], min_val=0, max_val=(NE - 1) * H)
                    pe.wait_ge(rt_t_ready, t + 1)
                    pe.matmul(bank[2 + (c + 1) % 2][:, 0:H], rt_t[:, (c + 1) % 2, :], w1_sb[:, cols(col, H)],
                              start=True, stop=True).then_inc(h_ready, 1)
                t = tau
                if not known or 0 <= t < TILES:
                    pe.wait_ge(h_biased, t + 1)
                    for j in range(HC):
                        m = pe.transpose(bank[4 + c % 2][:, j * P:(j + 1) * P],
                                         h_sb[:, c % 2, j * P:(j + 1) * P], ident[:, :])
                    m.then_inc(h_turned, 1)
                t = tau - 1
                if not known or t >= 0:
                    col = pe.value_load(tab_w[0:1, cols(t, 1)], min_val=0, max_val=(NE - 1) * H)
                    pe.wait_ge(h_t_ready, t + 1)
                    if not known or t >= 2:
                        pe.wait_ge(y_biased, t - 1)
                    for j in range(HC):
                        m = pe.matmul(bank[6 + (c + 1) % 2][:, 0:D], h_t[:, (c + 1) % 2, j * P:(j + 1) * P],
                                      w2_sb[:, cols(col + j * D, D)], start=(j == 0), stop=(j == HC - 1))
                    m.then_inc(y_ready, 1)

            pe.wait_ge(tables_ready, 1)
            pe.wait_ge(s_wexp, 32)
            tile_step(-1, 2)
            tile_step(-1, 3)
            tile_step(0, 0)
            for c in range(1, 5):
                tile_step(0, c)
            with pe.Fori(1, TILES // 4 - 1) as i:
                for c in range(1, 5):
                    tile_step(i, c)
            for c in range(1, 5):
                tile_step(TILES // 4 - 1, c)

        @block.scalar
        def _(act):
            def turned_evac(b, which):
                src, dst, done = ((turned1, xn_t, xn_t_ready), (turned2, x2n_t, x2n_t_ready))[which]
                for h in range(2):
                    act.wait_ge(src, 2 * b + h + 1)
                    act.activation(dst[:, h * HALF * P:(h + 1) * HALF * P], turn_ps[h][:, :], ACT.Copy
                                   ).then_inc(done, 1)

            def project_evac(b, par):
                act.wait_ge(norm_ready, b + 1)
                for t in range(T):
                    act.wait_ge(projected, T * b + t + 1)
                    act.activation(f_hom[:, t, :], proj_ps[t % 2][:, 0:D], ACT.Copy, scale=norm[:, par, t:t + 1])
                    act.activation(het_gate[:, par, t, :], proj_ps[t % 2][:, D:GN], ACT.Copy
                                   ).then_inc(proj_read, 1)

            def gate(b, par):
                act.wait_ge(gate_biased, b + 1)
                g = het_gate[:, par, :, D:2 * D]
                act.activation(g, g, ACT.Tanh, scale=0.5).then_inc(gate_ready, 1)

            def elu_exp(b, h):
                sl = slice(h * HALF, (h + 1) * HALF)
                act.wait_ge(z_ready, 2 * b + h + 1)
                act.activation(neg_sb[:, sl, :], z_sb[:, sl, :], ACT.Relu, scale=-1.0).then_inc(z_negated, 1)
                act.wait_ge(z_negated, 2 * b + h + 1)
                act.activation(neg_sb[:, sl, :], neg_sb[:, sl, :], ACT.Exp, scale=-1.0).then_inc(exp_ready, 1)

            def prob_exp(b):
                act.wait_ge(gaps_ready, b + 1)
                act.activation(p_exp[:, :], p_exp[:, :], ACT.Exp).then_inc(p_exp_ready, 1)

            def step(b, par, prev=True, nxt=True):
                gate(b, par)
                elu_exp(b, 0)
                if prev:
                    turned_evac(b - 1, 1)
                if nxt:
                    turned_evac(b + 1, 0)
                if prev:
                    prob_exp(b - 1)
                if nxt:
                    project_evac(b + 1, 1 - par)
                elu_exp(b, 1)

            turned_evac(0, 0)
            project_evac(0, 0)
            step(0, 0, prev=False)
            with act.Fori(0, B // 2 - 1) as i:
                step(2 * i + 1, 1)
                step(2 * i + 2, 0)
            step(B - 1, 1, nxt=False)
            turned_evac(B - 1, 1)
            prob_exp(B - 1)

            def tile_step(i, c):
                tau = 4 * i + c
                known = isinstance(tau, int)
                t = tau + 2
                if not known or t < TILES:
                    act.wait_ge(rt_turned, t + 1)
                    act.activation(rt_t[:, c % 2, :], bank[c % 2][:, 0:P], ACT.Copy).then_inc(rt_t_ready, 1)
                t = tau
                if not known or 0 <= t < TILES:
                    act.wait_ge(h_turned, t + 1)
                    act.activation(h_t[:, c % 2, :], bank[4 + c % 2][:, 0:H], ACT.Relu).then_inc(h_t_ready, 1)
                t = tau - 1
                if not known or t >= 0:
                    s = (c - 1) % 4
                    act.wait_ge(y_biased, t + 1)
                    if not known or t >= 4:
                        act.wait_ge(returned[s], 16 * (i + (c - 1) // 4))
                    act.activation(y_out[:, s, :], y_b[:, (c + 1) % 2, :], ACT.Copy,
                                   scale=rt[:, s, D + 1:D + 2]).then_inc(y_scaled, 1)

            tile_step(-1, 2)
            tile_step(-1, 3)
            tile_step(0, 0)
            for c in range(1, 5):
                tile_step(0, c)
            with act.Fori(1, TILES // 4 - 1) as i:
                for c in range(1, 5):
                    tile_step(i, c)
            for c in range(1, 5):
                tile_step(TILES // 4 - 1, c)

            with act.Fori(0, B) as b:
                act.wait_ge(out_ready, b + 1)
                act.dma_start(out[bass.ds(b, 1), :, :].rearrange("b p n -> (b p) n"), x1[:, cols(b * TD, TD)]
                              ).then_inc(stored, 16)
            act.wait_ge(stored, 16 * B)

        @block.vector
        def _(dve):
            steps = [0]

            def fresh():
                dve.sem_clear(dve_chain)
                steps[0] = 0

            def link(ins):
                steps[0] += 1
                ins.then_inc(dve_chain, 1)
                dve.wait_ge(dve_chain, steps[0])

            def layer_norm(b, par, ln, out_of, r=None):
                fresh()
                if ln == 0:
                    dve.wait_ge(x_loaded[par], 16 * (r + 1))
                for t in range(T):
                    last = dve.bn_stats(stats[:, ln, t, :], x1[:, cols(b * TD + t * D, D)])
                link(last)
                for t in range(T):
                    last = dve.bn_aggr(mean_var[:, ln, t, :], stats[:, ln, t, :])
                last.then_inc(stats_ready[ln], 1)

            def normalise(b, ln, out_of):
                dve.wait_ge(rstd_ready[ln], b + 1)
                for t in range(T):
                    last = dve.tensor_scalar(out_of(t), x1[:, cols(b * TD + t * D, D)], mean_var[:, ln, t, 0:1],
                                             rstd[:, ln, t:t + 1], ALU.subtract, ALU.mult)
                return last

            def xn_write(b):
                if not isinstance(b, int) or b >= 1:
                    dve.wait_ge(turned1, 2 * b)
                normalise(b, 0, lambda t: xn[:, t, :]).then_inc(xn_ready, 1)

            def column_sums(b, par, r):
                dve.wait_ge(adj_loaded[par], 64 * (r + 1))
                if not isinstance(b, int) or b >= 1:
                    dve.wait_ge(deg_summed, b)
                dve.tensor_reduce(col_sum_v[:, :], adj_sb[:, par, 0:5 * N].rearrange("p (c n) -> p n c", c=5),
                                  AX_X, ALU.add).then_inc(sum_v_ready, 1)

            def degree(b):
                dve.wait_ge(deg_summed, b + 1)
                dve.tensor_scalar(deg_sb[:, :], deg_ps, DEG_EPS, None, ALU.add).then_inc(deg_read, 1)

            def combine(b, par, h):
                sl = slice(h * HALF, (h + 1) * HALF)
                het = het_gate[:, par, sl, 0:D]
                th = het_gate[:, par, sl, D:2 * D]
                z = z_sb[:, sl, :]
                xb = x1[:, cols(b * TD + h * HALF * D, HALF * D)]
                fresh()
                dve.wait_ge(hom_ready, 2 * b + h + 1)
                for j in range(HALF):
                    t = h * HALF + j
                    last = dve.scalar_tensor_tensor(z_sb[:, t, :], hom_ps[h][:, j * P:(j + 1) * P],
                                                    norm[:, par, t:t + 1], het_gate[:, par, t, 0:D],
                                                    ALU.mult, ALU.subtract)
                last.then_inc(hom_read, 1)
                dve.wait_ge(hom_read, 2 * b + h + 1)
                dve.wait_ge(gate_ready, b + 1)
                link(dve.scalar_tensor_tensor(z, th, 1.0, z, ALU.add, ALU.mult))
                dve.scalar_tensor_tensor(z, z, 0.5, het, ALU.mult, ALU.add).then_inc(z_ready, 1)
                dve.wait_ge(exp_ready, 2 * b + h + 1)
                neg = neg_sb[:, sl, :]
                link(dve.scalar_tensor_tensor(z, z, 0.0, neg, ALU.max, ALU.add))
                link(dve.scalar_tensor_tensor(xb, z_sb[:, sl, :].rearrange("p t d -> p (t d)"), -1.0, xb,
                                              ALU.add, ALU.add))

            def route(b, par):
                fresh()
                dve.wait_ge(gated, b + 1)
                dve.tensor_tensor(scores[:, :, :], gate_ps.rearrange("p (t e) -> p t e", t=T),
                                  b_router_sb[:, :].rearrange("p (o e) -> p o e", o=1).broadcast_to((P, T, NE)),
                                  ALU.add).then_inc(scores_ready, 1)
                dve.wait_ge(pool_const, 1)
                dve.wait_ge(scores_ready, b + 1)
                for t in range(T):
                    last = dve.max(top[:, t, :], scores[:, t, :])
                link(last)
                dve.tensor_tensor(p_exp[:, :], top[:, :, 1], top[:, :, 0], ALU.subtract).then_inc(gaps_ready, 1)
                for t in range(T):
                    last = dve.max_index(top_at[:, t, :], top[:, t, :], scores[:, t, :])
                link(last)
                link(dve.tensor_copy(top_f[:, :, :], top_at[:, :, 0:K].rearrange("p t k -> p k t")))
                iota4 = iota_e[:, :].rearrange("p (k t e) -> p k t e", k=1, t=1).broadcast_to((P, K, T, NE))
                top4 = top_f[:, :, :].rearrange("p k (t o) -> p k t o", o=1).broadcast_to((P, K, T, NE))
                link(dve.tensor_tensor(chosen[:, :, :, :], iota4, top4, ALU.is_equal))
                dve.tensor_tensor(picked[:, :, :], chosen[:, 0, :, :], chosen[:, 1, :, :], ALU.add
                                  ).then_inc(picked_ready, 1)
                if not isinstance(b, int) or b >= 2:
                    r = (b - par) // 2 if isinstance(b, int) else None
                    dve.wait_ge(scattered[par], 16 * K * T * (r if r is not None else route_r[0]))
                dest = payload[:, par, :, :, D:D + 1].bitcast(I32)
                dve.tensor_scalar(dest, dest, float(2 * N), None, ALU.add)
                dve.wait_ge(p_exp_ready, b + 1)
                link(dve.tensor_scalar(p_sum[:, :], p_exp[:, :], 1.0, None, ALU.add))
                prob = [payload[:, par, k, :, D + 1] for k in range(K)]
                link(dve.reciprocal(prob[0], p_sum[:, :]))
                dve.tensor_tensor(prob[1], p_exp[:, :], prob[0], ALU.mult)

            def place_rows(b, par):
                fresh()
                dve.wait_ge(ranked, b + 1)
                nr = next_row[:, :].rearrange("p (o e) -> p o e", o=1).broadcast_to((P, T, NE))
                link(dve.tensor_tensor(place[:, :, :], rank_ps.rearrange("p (t e) -> p t e", t=T), nr, ALU.add))
                dve.tensor_tensor(next_row[:, :], next_row[:, :], total_ps, ALU.add)
                pl = place[:, :, :].rearrange("p (o t) e -> p o t e", o=1).broadcast_to((P, K, T, NE))
                link(dve.tensor_tensor(place_k[:, :, :, :], chosen[:, :, :, :], pl, ALU.mult))
                link(dve.tensor_reduce(slot_f[:, :, :], place_k[:, :, :, :], AX_X, ALU.add))
                dve.tensor_copy(slot[:, par, :, :], slot_f[:, :, :]).then_inc(slots_ready, 1)

            route_r = [None]

            def step(b, par, r, prev=True, nxt=True):
                if nxt:
                    layer_norm(b + 1, 1 - par, 0, None, r + par)
                    column_sums(b + 1, 1 - par, r + par)
                    xn_write(b + 1)
                combine(b, par, 0)
                if prev:
                    route_r[0] = r - 1 + par
                    route(b - 1, 1 - par)
                    place_rows(b - 1, 1 - par)
                if nxt:
                    degree(b + 1)
                combine(b, par, 1)
                layer_norm(b, par, 1, None)
                if not isinstance(b, int) or b >= 2:
                    dve.wait_ge(scattered[par], 16 * K * T * r)
                normalise(b, 1, lambda t: payload[:, par, 0, t, 0:D]).then_inc(x2n_ready, 1)

            dve.wait_ge(pool_const, 1)
            dve.wait_ge(s_const, 64)
            layer_norm(0, 0, 0, None, 0)
            column_sums(0, 0, 0)
            xn_write(0)
            degree(0)
            step(0, 0, 0, prev=False)
            with dve.Fori(0, B // 2 - 1) as i:
                step(2 * i + 1, 1, i)
                step(2 * i + 2, 0, i + 1)
            step(B - 1, 1, B // 2 - 1, nxt=False)
            route(B - 1, 1)
            place_rows(B - 1, 1)

            dve.wait_ge(slots_ready, B)
            dve.wait_ge(iotas, 1)
            dve.tensor_scalar(pad_slot, next_row[:, :], part_iota[:, 0:1], None, ALU.add).then_inc(pad_slots_ready, 1)
            fresh()
            for e in range(NE):
                last = dve.tensor_scalar(count_i[:, e:e + 1], next_row[:, e:e + 1], float(P - 1 - e * REG), None,
                                         ALU.add)
            link(last)
            link(dve.tensor_scalar(count_i[:, :], count_i[:, :], 7, None, ALU.logical_shift_right))
            link(dve.tensor_copy(tiles_e[:, :], count_i[:, :]))
            link(dve.tensor_copy(tiles_end[:, 0:1], tiles_e[:, 0:1]))
            for e in range(1, NE):
                link(dve.tensor_tensor(tiles_end[:, e:e + 1], tiles_end[:, e - 1:e], tiles_e[:, e:e + 1], ALU.add))
            link(dve.tensor_scalar(skip_e[:, :], tiles_e[:, :], -float(P), float(REG), ALU.mult, ALU.add))
            dve.tensor_scalar(tile_e[:, :], tile_iota, tiles_end[:, 0:1], None, ALU.is_ge)
            link(dve.tensor_scalar(tile_row[:, :], tile_iota, float(P), None, ALU.mult))
            for e in range(NE):
                if e:
                    dve.scalar_tensor_tensor(tile_e[:, :], tile_iota, tiles_end[:, e:e + 1], tile_e[:, :],
                                             ALU.is_ge, ALU.add)
                link(dve.tensor_scalar(reach[:, :], tile_iota, tiles_end[:, e:e + 1], skip_e[:, e:e + 1],
                                       ALU.is_ge, ALU.mult))
                link(dve.tensor_tensor(tile_row[:, :], tile_row[:, :], reach[:, :], ALU.add))
            link(dve.tensor_scalar(tile_e[:, :], tile_e[:, :], float(NE - 1), None, ALU.min))
            dve.tensor_scalar(tab_w[:, :], tile_e[:, :], float(H), None, ALU.mult)
            dve.tensor_scalar(tab_b[:, :], tile_e[:, :], float(EB), None, ALU.mult)
            dve.tensor_copy(tab_row[:, :], tile_row[:, :]).then_inc(tables_ready, 1)
            dve.wait_ge(tables_ready, 1)
            dve.wait_ge(s_bias, 16)

            def tile_step(i, c):
                tau = 4 * i + c
                known = isinstance(tau, int)
                t = tau + 1
                if not known or 0 <= t < TILES:
                    col = dve.value_load(tab_b[0:1, cols(t, 1)], min_val=0, max_val=(NE - 1) * EB)
                    dve.wait_ge(h_ready, t + 1)
                    dve.tensor_tensor(h_sb[:, (c + 1) % 2, :], bank[2 + (c + 1) % 2][:, 0:H],
                                      bias_sb[:, cols(col, H)], ALU.add).then_inc(h_biased, 1)
                t = tau - 1
                if not known or t >= 0:
                    col = dve.value_load(tab_b[0:1, cols(t, 1)], min_val=0, max_val=(NE - 1) * EB)
                    dve.wait_ge(y_ready, t + 1)
                    if not known or t >= 2:
                        dve.wait_ge(y_scaled, t - 1)
                    dve.tensor_tensor(y_b[:, (c + 1) % 2, :], bank[6 + (c + 1) % 2][:, 0:D],
                                      bias_sb[:, cols(col + H, D)], ALU.add).then_inc(y_biased, 1)

            tile_step(-1, 3)
            tile_step(0, 0)
            for c in range(1, 5):
                tile_step(0, c)
            with dve.Fori(1, TILES // 4 - 1) as i:
                for c in range(1, 5):
                    tile_step(i, c)
            for c in range(1, 5):
                tile_step(TILES // 4 - 1, c)

            with dve.Fori(0, B // 2) as r:
                for par in range(2):
                    b = 2 * r + par
                    fresh()
                    dve.wait_ge(y_loaded[par], 16 * K * (r + 1))
                    xb = x1[:, cols(b * TD, TD)]
                    link(dve.tensor_tensor(y_in[:, par, 0, :], y_in[:, par, 0, :], y_in[:, par, 1, :], ALU.add))
                    dve.tensor_tensor(xb, xb, y_in[:, par, 0, :], ALU.add).then_inc(out_ready, 1)


def kernel(x, adj, L0_gnn_W_t, L0_gnn_b_t, L0_gnn_W_h, L0_gnn_theta, L0_ffn_Wg, L0_ffn_bg, L0_ffn_W1, L0_ffn_b1,
           L0_ffn_W2, L0_ffn_b2):
    import numpy as np
    import concourse.bacc as bacc
    from concourse.bass_utils import run_bass_kernel_spmd as launch

    b, n, d = x.shape
    t = n // P
    ne, h, _ = L0_ffn_W1.shape
    c = np.ascontiguousarray
    rows = lambda a: c(np.broadcast_to(np.asarray(a).reshape(1, -1), (P, a.size)))
    adj_t = np.asarray(adj).reshape(b, P, t, P, t).transpose(0, 3, 4, 2, 1)
    w2_t = np.asarray(L0_ffn_W2).reshape(ne, d, h // P, P).transpose(3, 0, 2, 1)
    arrays = {
        "x": c(np.asarray(x).reshape(b, P, t * d)),
        "adj_t": c(adj_t).reshape(b, P, t * n),
        "w_gnn": c(np.concatenate([np.asarray(L0_gnn_theta), np.asarray(L0_gnn_W_h), np.asarray(L0_gnn_W_t)], 1)),
        "b_gate": rows(np.asarray(L0_gnn_b_t)),
        "wg_t": c(np.asarray(L0_ffn_Wg).T),
        "b_router": rows(np.asarray(L0_ffn_bg)),
        "w1_t": c(np.asarray(L0_ffn_W1).transpose(2, 0, 1)).reshape(d, ne * h),
        "w2_t": c(w2_t).reshape(P, ne * h),
        "bias_e": rows(np.concatenate([np.asarray(L0_ffn_b1), np.asarray(L0_ffn_b2)], 1)),
    }
    nc = bacc.Bacc("TRN2", target_bir_lowering=False, num_devices=1)
    args = [nc.dram_tensor(f"in_{k}", a.shape, F32, kind="ExternalInput").ap() for k, a in arrays.items()]
    out = nc.dram_tensor("out", (b, P, t * d), F32, kind="ExternalOutput").ap()
    build(nc, *args, out)
    got = launch(nc, [{f"in_{k}": a for k, a in arrays.items()}], core_ids=[0])
    return got.results[0]["out"].reshape(b, n, d)
```

```python
from contextlib import ExitStack

import concourse.bass as bass
from concourse import mybir

F32 = mybir.dt.float32
BF16 = mybir.dt.bfloat16
I32 = mybir.dt.int32
U32 = mybir.dt.uint32
ALU = mybir.AluOpType
ACT = mybir.ActivationFunctionType
AX_X = mybir.AxisListType.X

P = 128
EPS = 1e-5
DEG_EPS = 1e-6


def build(nc, x, x_t, adj_t, w_gnn, b_gate, wg_t, b_router, w1b_t, w2_t, b2, out):
    B, _, TD = x.shape
    D = P
    T = TD // D
    N = P * T
    NE = wg_t.shape[1]
    H = w2_t.shape[1] // NE
    HC = H // P
    WB = H + HC
    K = 2
    TOK = B * N
    REG = TOK + P
    FULL = K * TOK // P
    TILES = FULL + NE
    SPARE = TILES - FULL
    ROW = D + 2
    GN = 3 * D
    R, W = 8, 4
    HALF = T // 2

    routed = nc.dram_tensor("routed", (NE * REG + SPARE * P, ROW), F32, kind="Internal").ap()
    expert_out = nc.dram_tensor("expert_out", (K * TOK + (NE + SPARE) * P, D), F32, kind="Internal").ap()
    expert_out_kb = expert_out[0:K * TOK, :].rearrange("(k b p t) d -> k b p (t d)", k=K, b=B, p=P)

    with ExitStack() as ctx:
        def sb(name, shape, dt=F32):
            return ctx.enter_context(nc.sbuf_tensor(name, shape, dt))

        def ps(name, shape):
            return ctx.enter_context(nc.psum_tensor(name, shape, F32))

        def sem(name):
            return ctx.enter_context(nc.semaphore(name))

        w_raw = sb("w_raw", [P, GN])
        w_gnn_sb = sb("w_gnn_sb", [P, GN])
        wg_sb = sb("wg_sb", [P, NE])
        b_gate_sb = sb("b_gate_sb", [P, D])
        b_router_sb = sb("b_router_sb", [P, NE])
        w2_sb = sb("w2_sb", [P, NE * H])
        ident = sb("ident", [P, P])
        ones_f = sb("ones_f", [P, P])
        before = sb("before", [P, P], BF16)
        ones_bf = sb("ones_bf", [P, P], BF16)
        iota_e = sb("iota_e", [P, NE])
        minus_half = sb("minus_half", [P, T])

        adj_sb = sb("adj_sb", [P, 2, T * N])
        x1 = sb("x1", [P, B * TD])
        x_t_sb = sb("x_t_sb", [P, 2, N])
        f_hom = sb("f_hom", [P, T, D])
        het_gate = sb("het_gate", [P, 2, T, 2 * D])
        col_sum = sb("col_sum", [P, N])
        x2n_t = sb("x2n_t", [P, N])
        z_sb = sb("z_sb", [P, T, D])
        neg_sb = sb("neg_sb", [P, T, D])
        stats = sb("stats", [P, 2, T, 6])
        mean_var = sb("mean_var", [P, 2, T, 2])
        rstd = sb("rstd", [P, 2, T])
        deg_sb = sb("deg_sb", [P, T])
        norm = sb("norm", [P, 2, T])
        rstd_norm = sb("rstd_norm", [P, T])
        shift = sb("shift", [P, T])
        payload = sb("payload", [P, 2, K, T, ROW])
        scores = sb("scores", [P, T, NE])
        top = sb("top", [P, T, 8])
        top_at = sb("top_at", [P, T, 8], U32)
        top_f = sb("top_f", [P, K, T])
        chosen = sb("chosen", [P, K, T, NE])
        picked = sb("picked", [P, T, NE], BF16)
        place = sb("place", [P, T, NE])
        place_k = sb("place_k", [P, K, T, NE])
        slot_f = sb("slot_f", [P, K, T])
        slot = sb("slot", [P, 2, K, T], I32)
        next_row = sb("next_row", [P, NE])
        p_exp = sb("p_exp", [P, T])
        p_sum = sb("p_sum", [P, T])

        used = [0, 0]

        def in_adj(buf, n):
            at = used[buf]
            used[buf] += n
            assert used[buf] <= T * N
            return adj_sb[:, buf, at:at + n]

        b2_sb = in_adj(0, NE * D)
        pad_rows = in_adj(0, NE * ROW).rearrange("p (e r) -> p e r", r=ROW)
        spare_rows = in_adj(0, SPARE * ROW).rearrange("p (e r) -> p e r", r=ROW)
        pad_slot = in_adj(0, NE).bitcast(I32)
        y_in = in_adj(0, 2 * K * TD).rearrange("p (s k n) -> p s k n", s=2, k=K)
        tile_iota = in_adj(1, TILES)
        rt = in_adj(1, R * ROW).rearrange("p (s r) -> p s r", r=ROW)
        w1 = in_adj(1, W * WB).rearrange("p (s n) -> p s n", s=W)
        rt_t = in_adj(1, 2 * P).rearrange("p (s n) -> p s n", s=2)
        h_t = in_adj(1, 2 * H).rearrange("p (s n) -> p s n", s=2)
        y_b = in_adj(1, 2 * D).rearrange("p (s n) -> p s n", s=2)
        y_out = in_adj(1, R * D).rearrange("p (s n) -> p s n", s=R)
        dest = in_adj(1, R).bitcast(I32)
        part_iota = sb("part_iota", [P, 1])
        count_i = sb("count_i", [P, NE], I32)
        tiles_e = sb("tiles_e", [P, NE])
        tiles_end = sb("tiles_end", [P, NE])
        skip_e = sb("skip_e", [P, NE])
        reach = sb("reach", [P, TILES])
        tile_e = sb("tile_e", [P, TILES])
        tile_row = sb("tile_row", [P, TILES])
        tab_w2 = sb("tab_w2", [P, TILES], I32)
        tab_e = sb("tab_e", [P, TILES], I32)
        tab_row = sb("tab_row", [P, TILES], I32)

        bank = [ps(f"bank{i}", [P, 512]) for i in range(8)]
        hom_ps = bank[0:2]
        turn_ps = bank[2:4]
        proj_ps = bank[4:6]
        w_sum_ps = bank[7][:, 0:GN]
        gate_ps, deg_ps = bank[6][:, 0:T * NE], bank[6][:, 128:128 + T]
        rank_ps, total_ps = bank[7][:, 0:T * NE], bank[7][:, 128:128 + NE]

        s_const = sem("s_const")
        s_wexp = sem("s_wexp")
        s_bias = sem("s_bias")
        x_loaded = [sem(f"x_loaded{i}") for i in range(2)]
        adj_loaded = [sem(f"adj_loaded{i}") for i in range(2)]
        iotas = sem("iotas")
        pool_const = sem("pool_const")
        dve_const = sem("dve_const")
        stats_ready = [sem(f"stats_ready{i}") for i in range(2)]
        rstd_ready = [sem(f"rstd_ready{i}") for i in range(2)]
        w_summed, w_centred = sem("w_summed"), sem("w_centred")
        turned, x2n_t_ready = sem("turned"), sem("x2n_t_ready")
        sum_ready = sem("sum_ready")
        deg_summed, deg_read, norm_ready = sem("deg_summed"), sem("deg_read"), sem("norm_ready")
        projected, proj_read = sem("projected"), sem("proj_read")
        gate_biased, gate_ready = sem("gate_biased"), sem("gate_ready")
        hom_ready, hom_read = sem("hom_ready"), sem("hom_read")
        x1_ready = sem("x1_ready")
        z_ready, z_negated, exp_ready = sem("z_ready"), sem("z_negated"), sem("exp_ready")
        x2n_ready = sem("x2n_ready")
        gated, scores_ready, gaps_ready = sem("gated"), sem("scores_ready"), sem("gaps_ready")
        picked_ready, ranked, ranks_read = sem("picked_ready"), sem("ranked"), sem("ranks_read")
        p_exp_ready = sem("p_exp_ready")
        slots_ready, shift_ready, copied = sem("slots_ready"), sem("shift_ready"), sem("copied")
        scattered = [sem(f"scattered{i}") for i in range(2)]
        dve_chain, pool_chain = sem("dve_chain"), sem("pool_chain")
        dve_waits, pool_waits = sem("dve_waits"), sem("pool_waits")
        spares_written = sem("spares_written")
        pads_ready, pads_written = sem("pads_ready"), sem("pads_written")
        pad_slots_ready, tables_ready = sem("pad_slots_ready"), sem("tables_ready")
        rt_loaded = [sem(f"rt_loaded{i}") for i in range(R)]
        w1_loaded = [sem(f"w1_loaded{i}") for i in range(W)]
        rt_turned, rt_t_ready = sem("rt_turned"), sem("rt_t_ready")
        h_ready = [sem("h_ready_act"), sem("h_ready_dve")]
        h_t_ready = [sem("h_t_ready_act"), sem("h_t_ready_dve")]
        y_ready, y_biased, y_scaled = sem("y_ready"), sem("y_biased"), sem("y_scaled")
        returned = [sem(f"returned{i}") for i in range(R)]
        y_loaded = [sem(f"y_loaded{i}") for i in range(2)]
        out_ready = sem("out_ready")
        stored = sem("stored")

        assert P == D, "a tile's table entry tab_e serves rows of w1b_t and columns of b2_sb"
        block = ctx.enter_context(nc.Block())

        def run_tiles(eng, tile_step, first):
            for c in range(R + first, R):
                tile_step(-1, c)
            tile_step(0, 0)
            for c in range(1, R + 1):
                tile_step(0, c)
            with eng.Fori(1, TILES // R - 1) as i:
                for c in range(1, R + 1):
                    tile_step(i, c)
            for c in range(1, R + 1):
                tile_step(TILES // R - 1, c)
        QTR = T * N // 4

        def cols(at, n):
            return bass.ds(at, n)

        @block.sync
        def _(sp):
            def load(b, par, r):
                if not isinstance(b, int) or b >= 2:
                    sp.wait_ge(hom_ready, 2 * (b - 1))
                sp.dma_start(x1[:, cols(b * TD, TD)], x[bass.ds(b, 1), :, :].rearrange("b p n -> (b p) n")
                             ).then_inc(x_loaded[par], 16)
                sp.dma_start(x_t_sb[:, par, :], x_t[bass.ds(b, 1), :, :].rearrange("b p n -> (b p) n")
                             ).then_inc(x_loaded[par], 16)
                for q in range(4):
                    sp.dma_start(adj_sb[:, par, q * QTR:(q + 1) * QTR],
                                 adj_t[bass.ds(b, 1), :, q * QTR:(q + 1) * QTR].rearrange("b p n -> (b p) n")
                                 ).then_inc(adj_loaded[par], 16)

            load(0, 0, 0)
            for dst, src in ((w_raw, w_gnn), (b_gate_sb, b_gate), (wg_sb, wg_t), (b_router_sb, b_router)):
                sp.dma_start(dst[:, :], src).then_inc(s_const, 16)
            load(1, 1, 0)
            sp.dma_start(w2_sb[:, :], w2_t).then_inc(s_wexp, 16)
            with sp.Fori(1, B // 2) as r:
                load(2 * r, 0, r)
                load(2 * r + 1, 1, r)
            sp.wait_ge(hom_ready, 2 * (B - 1))
            sp.dma_start(b2_sb, b2).then_inc(s_bias, 16)
            sp.wait_ge(pads_ready, 1)
            for j in range(SPARE):
                sp.dma_start(routed[NE * REG + j * P:NE * REG + (j + 1) * P, :], spare_rows[:, j, :]
                             ).then_inc(spares_written, 16)

            sp.wait_ge(tables_ready, 1)
            for par in range(2):
                sp.wait_ge(scattered[par], 16 * K * T * B // 2)
            sp.wait_ge(pads_written, 16 * NE)
            sp.wait_ge(spares_written, 16 * SPARE)

            def load_tile(t, s):
                row = sp.value_load(tab_row[0:1, cols(t, 1)], min_val=0, max_val=NE * REG + (SPARE - 1) * P)
                sp.dma_start(rt[:, s, :], routed[bass.ds(row, P), :]).then_inc(rt_loaded[s], 16)
                e = sp.value_load(tab_e[0:1, cols(t, 1)], min_val=0, max_val=(NE - 1) * P)
                if not isinstance(t, int) or t >= W:
                    sp.wait_ge(h_t_ready[0], t - W + 1)
                    sp.wait_ge(h_t_ready[1], t - W + 1)
                sp.dma_start(w1[:, s % W, :], w1b_t[bass.ds(e, P), :]).then_inc(w1_loaded[s % W], 16)

            for t in range(R):
                load_tile(t, t)
            with sp.Fori(1, TILES // R) as i:
                for s in range(R):
                    sp.wait_ge(y_scaled, R * (i - 1) + s + 1)
                    load_tile(R * i + s, s)
            for s in range(R):
                sp.wait_ge(returned[s], 16 * (TILES // R))

            def load_y(b, par):
                for k in range(K):
                    sp.dma_start(y_in[:, par, k, :],
                                 expert_out_kb[k, bass.ds(b, 1), :, :].rearrange("b p n -> (b p) n")
                                 ).then_inc(y_loaded[par], 16)

            load_y(0, 0)
            load_y(1, 1)
            with sp.Fori(1, B // 2) as r:
                for par in range(2):
                    sp.wait_ge(out_ready, 2 * (r - 1) + par + 1)
                    load_y(2 * r + par, par)

        @block.gpsimd
        def _(pool):
            pool.memset(ident[:, :], 0.0).then_inc(pool_chain, 1)
            pool.memset(ones_bf[:, :], 1.0).then_inc(pool_chain, 1)
            pool.memset(ones_f[:, :], 1.0)
            pool.memset(minus_half[:, :], -0.5)
            pool.wait_ge(pool_chain, 2)
            pool.affine_select(out=ident[:, :], in_=ident[:, :], compare_op=ALU.not_equal, fill=1.0, base=0,
                               pattern=[[-1, P]], channel_multiplier=1)
            pool.affine_select(out=before[:, :], in_=ones_bf[:, :], compare_op=ALU.is_gt, fill=0.0, base=0,
                               pattern=[[1, P]], channel_multiplier=-1)
            pool.iota(iota_e[:, :], pattern=[[1, NE]], base=0, channel_multiplier=0,
                      allow_small_or_imprecise_dtypes=True)
            pool.iota(next_row[:, :], pattern=[[REG, NE]], base=0, channel_multiplier=0,
                      allow_small_or_imprecise_dtypes=True)
            pool.iota(part_iota[:, :], pattern=[[0, 1]], base=0, channel_multiplier=1,
                      allow_small_or_imprecise_dtypes=True)
            for par in range(2):
                last = pool.iota(payload[:, par, :, :, D:D + 1].bitcast(I32), pattern=[[TOK, K], [1, T], [0, 1]], base=(par - 2) * N,
                                 channel_multiplier=T)
            last.then_inc(pool_const, 1)

            def held():
                pool.sem_inc(pool_waits, 1)

            def rstd_of(ln, b):
                pool.sem_clear(pool_chain)
                pool.wait_ge(stats_ready[ln], b + 1)
                held()
                pool.tensor_scalar(rstd[:, ln, :], mean_var[:, ln, :, 1], EPS, None, ALU.add).then_inc(pool_chain, 1)
                pool.wait_ge(pool_chain, 1)
                pool.tensor_tensor(rstd[:, ln, :], rstd[:, ln, :], minus_half[:, :], ALU.pow
                                   ).then_inc(rstd_ready[ln], 1)

            def degree_norm(b, par):
                pool.sem_clear(pool_chain)
                pool.wait_ge(deg_read, b + 1)
                pool.tensor_tensor(norm[:, par, :], deg_sb[:, :], minus_half[:, :], ALU.pow).then_inc(pool_chain, 1)
                pool.wait_ge(pool_chain, 1)
                if not isinstance(b, int) or b >= 1:
                    pool.wait_ge(proj_read, T * b)
                pool.tensor_tensor(rstd_norm[:, :], norm[:, par, :], rstd[:, 0, :], ALU.mult).then_inc(norm_ready, 1)

            def second_shift(b):
                pool.sem_clear(pool_chain)
                pool.wait_ge(rstd_ready[1], b + 1)
                pool.tensor_tensor(shift[:, :], mean_var[:, 1, :, 0], rstd[:, 1, :], ALU.mult
                                   ).then_inc(pool_chain, 1)
                pool.wait_ge(pool_chain, 1)
                pool.tensor_scalar(shift[:, :], shift[:, :], -1.0, None, ALU.mult).then_inc(shift_ready, 1)

            def scatter(b, par, which, first=False):
                if first:
                    pool.wait_ge(slots_ready, b + 1)
                    held()
                for n in which:
                    k, t = n // T, n % T
                    pool.indirect_dma_start(
                        routed[:, :], bass.IndirectOffsetOnAxis(ap=slot[:, par, k, t:t + 1], axis=0),
                        payload[:, par, k, t, :], None).then_inc(scattered[par], 16)

            def step(b, par, prev=1, nxt=True):
                if nxt:
                    rstd_of(0, b + 1)
                if prev > 1:
                    scatter(b - 2, par, range(6, K * T))
                if nxt:
                    degree_norm(b + 1, 1 - par)
                if prev:
                    scatter(b - 1, 1 - par, range(0, 4), first=True)
                rstd_of(1, b)
                second_shift(b)
                if prev:
                    scatter(b - 1, 1 - par, range(4, 6))

            rstd_of(0, 0)
            degree_norm(0, 0)
            step(0, 0, prev=0)
            step(1, 1, prev=1)
            step(2, 0, prev=2)
            with pool.Fori(1, B // 2 - 1) as i:
                step(2 * i + 1, 1, prev=2)
                step(2 * i + 2, 0, prev=2)
            step(B - 1, 1, prev=2, nxt=False)
            scatter(B - 2, 0, range(6, K * T))
            pool.wait_ge(hom_ready, 2 * B)
            pool.sem_clear(pool_chain)
            pool.memset(pad_rows, 0.0).then_inc(pool_chain, 1)
            pool.memset(spare_rows, 0.0).then_inc(pool_chain, 1)
            pool.wait_ge(pool_chain, 2)
            pool.iota(pad_rows[:, :, D:D + 1].bitcast(I32), pattern=[[P, NE], [0, 1]], base=K * TOK,
                      channel_multiplier=1)
            pool.iota(spare_rows[:, :, D:D + 1].bitcast(I32), pattern=[[P, SPARE], [0, 1]],
                      base=K * TOK + NE * P, channel_multiplier=1).then_inc(pads_ready, 1)
            pool.iota(tile_iota, pattern=[[1, TILES]], base=0, channel_multiplier=0,
                      allow_small_or_imprecise_dtypes=True).then_inc(iotas, 1)
            scatter(B - 1, 1, range(K * T), first=True)
            pool.wait_ge(pads_ready, 1)
            pool.wait_ge(pad_slots_ready, 1)
            for e in range(NE):
                pool.indirect_dma_start(
                    routed[:, :], bass.IndirectOffsetOnAxis(ap=pad_slot[:, e:e + 1], axis=0),
                    pad_rows[:, e, :], None).then_inc(pads_written, 16)

            def send(t, s):
                pool.wait_ge(y_scaled, t + 1)
                held()
                pool.indirect_dma_start(
                    expert_out[:, :], bass.IndirectOffsetOnAxis(ap=dest[:, s:s + 1], axis=0),
                    y_out[:, s, :], None).then_inc(returned[s], 16)

            with pool.Fori(0, TILES // R) as i:
                for s in range(R):
                    send(R * i + s, s)

        @block.tensor
        def _(pe):
            def turn_x2n(b, par):
                pe.wait_ge(x2n_ready, b + 1)
                for h in range(2):
                    if not isinstance(b, int) or b >= 1:
                        pe.wait_ge(x2n_t_ready, 2 * (b - 1) + h + 1)
                    for j in range(HALF):
                        m = pe.transpose(turn_ps[h][:, j * P:(j + 1) * P],
                                         payload[:, par, 0, h * HALF + j, 0:D], ident[:, :])
                    m.then_inc(turned, 1)

            def router(b):
                pe.wait_ge(x2n_t_ready, 2 * (b + 1))
                pe.wait_ge(deg_read, min(b + 2, B) if isinstance(b, int) else b + 2)
                for t in range(T):
                    m = pe.matmul(gate_ps[:, t * NE:(t + 1) * NE], x2n_t[:, t * P:(t + 1) * P], wg_sb[:, :],
                                  start=True, stop=True)
                m.then_inc(gated, 1)

            def ranks(b):
                pe.wait_ge(picked_ready, b + 1)
                flat = picked[:, :, :].rearrange("p t e -> p (t e)")
                pe.matmul(rank_ps, before[:, :], flat, start=True, stop=False, skip_group_check=True)
                for s in range(1, T):
                    pe.matmul(rank_ps[:, s * NE:], ones_bf[:, :], flat[:, 0:(T - s) * NE], start=False,
                              stop=(s == T - 1), skip_group_check=True)
                for t in range(T):
                    m = pe.matmul(total_ps, ones_bf[:, :], picked[:, t, :], start=(t == 0), stop=(t == T - 1),
                                  skip_group_check=True)
                m.then_inc(ranked, 1)

            def degree(b):
                pe.wait_ge(sum_ready, b + 1)
                if not isinstance(b, int) or b >= 2:
                    pe.wait_ge(scores_ready, b - 1)
                for t in range(T):
                    m = pe.matmul(deg_ps[:, t:t + 1], col_sum[:, t * P:(t + 1) * P], ones_f[:, 0:1],
                                  start=True, stop=True)
                m.then_inc(deg_summed, 1)

            def project(b, par, r):
                pe.wait_ge(x_loaded[par], 32 * (r + 1))
                for t in range(T):
                    if not isinstance(b, int) or b * T + t >= 2:
                        pe.wait_ge(proj_read, T * b + t - 1)
                    pe.matmul(proj_ps[t % 2][:, 0:GN], x_t_sb[:, par, t * P:(t + 1) * P], w_gnn_sb[:, :],
                              start=True, stop=True).then_inc(projected, 1)

            def aggregate(b, par, tiles, wait=False, done=False):
                h = tiles[0] // HALF
                if wait:
                    if not isinstance(b, int) or b >= 1:
                        pe.wait_ge(hom_read, 2 * (b - 1) + h + 1)
                for t in tiles:
                    for c in range(T):
                        if t == 0:
                            pe.wait_ge(proj_read, T * b + c + 1)
                        at = (c * T + t) * P
                        m = pe.matmul(hom_ps[h][:, (t % HALF) * P:(t % HALF + 1) * P], adj_sb[:, par, at:at + P],
                                      f_hom[:, c, :], start=(c == 0), stop=(c == T - 1))
                if done:
                    m.then_inc(hom_ready, 1)

            def step(b, par, r, prev=True, nxt=True):
                aggregate(b, par, range(0, HALF), wait=True, done=True)
                if prev:
                    turn_x2n(b - 1, 1 - par)
                    router(b - 1)
                aggregate(b, par, range(HALF, T - 2), wait=True)
                if prev:
                    ranks(b - 1)
                aggregate(b, par, range(T - 2, T), done=True)
                if nxt:
                    degree(b + 1)
                    project(b + 1, 1 - par, r + par)

            pe.wait_ge(pool_const, 1)
            pe.wait_ge(s_const, 64)
            pe.matmul(w_sum_ps, ones_f[:, :], w_raw[:, :], start=True, stop=True).then_inc(w_summed, 1)
            pe.wait_ge(w_centred, 1)
            degree(0)
            project(0, 0, 0)
            step(0, 0, 0, prev=False)
            step(1, 1, 0)
            step(2, 0, 1)
            with pe.Fori(1, B // 2 - 1) as i:
                step(2 * i + 1, 1, i)
                step(2 * i + 2, 0, i + 1)
            step(B - 1, 1, B // 2 - 1, nxt=False)
            turn_x2n(B - 1, 1)
            router(B - 1)
            ranks(B - 1)

            def tile_step(i, c):
                tau = R * i + c
                known = isinstance(tau, int)
                t = tau + 2
                if not known or t < TILES:
                    s = (c + 2) % R
                    pe.wait_ge(rt_loaded[s], 16 * (i + (c + 2) // R + 1))
                    pe.transpose(bank[c % 2][:, 0:P], rt[:, s, 0:D], ident[:, :]).then_inc(rt_turned, 1)
                t = tau - 1
                if not known or t >= 0:
                    col = pe.value_load(tab_w2[0:1, cols(t, 1)], min_val=0, max_val=(NE - 1) * H)
                    for half in range(2):
                        pe.wait_ge(h_t_ready[half], t + 1)
                    if not known or t >= 2:
                        pe.wait_ge(y_biased, t - 1)
                    for j in range(HC):
                        m = pe.matmul(bank[6 + (c + 1) % 2][:, 0:D], h_t[:, (c + 1) % 2, j * P:(j + 1) * P],
                                      w2_sb[:, cols(col + j * D, D)], start=(j == 0), stop=(j == HC - 1))
                    m.then_inc(y_ready, 1)
                t = tau + 1
                if not known or 0 <= t < TILES:
                    pe.wait_ge(w1_loaded[(c + 1) % W], 16 * (R // W * i + (c + 1) // W + 1))
                    pe.wait_ge(rt_t_ready, t + 1)
                    for half in range(2):
                        for j in range(HC // 2):
                            n = half * HC // 2 + j
                            m = pe.matmul(bank[2 + 2 * ((c + 1) % 2) + half][:, j * P:(j + 1) * P],
                                          w1[:, (c + 1) % W, n * P:(n + 1) * P], rt_t[:, (c + 1) % 2, :],
                                          start=True, stop=True)
                        m.then_inc(h_ready[half], 1)

            pe.wait_ge(tables_ready, 1)
            pe.wait_ge(s_wexp, 16)
            run_tiles(pe, tile_step, -2)

        @block.scalar
        def _(act):
            def turned_evac(b):
                for h in range(2):
                    act.wait_ge(turned, 2 * b + h + 1)
                    act.activation(x2n_t[:, h * HALF * P:(h + 1) * HALF * P], turn_ps[h][:, :], ACT.Copy
                                   ).then_inc(x2n_t_ready, 1)

            def project_evac(b, par):
                act.wait_ge(norm_ready, b + 1)
                for t in range(T):
                    act.wait_ge(projected, T * b + t + 1)
                    act.activation(f_hom[:, t, :], proj_ps[t % 2][:, 0:D], ACT.Copy, scale=rstd_norm[:, t:t + 1])
                    act.activation(het_gate[:, par, t, :], proj_ps[t % 2][:, D:GN], ACT.Copy,
                                   scale=rstd[:, 0, t:t + 1]).then_inc(proj_read, 1)

            def hom_evac(b, par, h):
                act.wait_ge(hom_ready, 2 * b + h + 1)
                if h == 0:
                    if not isinstance(b, int) or b >= 1:
                        act.wait_ge(x1_ready, 2 * b)
                for j in range(HALF):
                    t = h * HALF + j
                    m = act.activation(z_sb[:, t, :], hom_ps[h][:, j * P:(j + 1) * P], ACT.Copy,
                                       scale=norm[:, par, t:t + 1])
                m.then_inc(hom_read, 1)

            def second_norm(b, par, r):
                act.wait_ge(shift_ready, b + 1)
                if not isinstance(b, int) or b >= 2:
                    act.wait_ge(scattered[par], 16 * K * T * r)
                for t in range(T):
                    m = act.activation(payload[:, par, 0, t, 0:D], x1[:, cols(b * TD + t * D, D)], ACT.Identity,
                                       bias=shift[:, t:t + 1], scale=rstd[:, 1, t:t + 1])
                m.then_inc(x2n_ready, 1)
                act.wait_ge(x2n_ready, b + 1)
                act.activation(payload[:, par, 1, :, 0:D], payload[:, par, 0, :, 0:D], ACT.Copy
                               ).then_inc(copied, 1)

            def gate(b, par):
                act.wait_ge(gate_biased, b + 1)
                g = het_gate[:, par, :, D:2 * D]
                act.activation(g, g, ACT.Tanh, scale=0.5).then_inc(gate_ready, 1)

            def elu_exp(b, h):
                sl = slice(h * HALF, (h + 1) * HALF)
                act.wait_ge(z_ready, 2 * b + h + 1)
                act.activation(neg_sb[:, sl, :], z_sb[:, sl, :], ACT.Relu, scale=-1.0).then_inc(z_negated, 1)
                act.wait_ge(z_negated, 2 * b + h + 1)
                act.activation(neg_sb[:, sl, :], neg_sb[:, sl, :], ACT.Exp, scale=-1.0).then_inc(exp_ready, 1)

            def prob_exp(b):
                act.wait_ge(gaps_ready, b + 1)
                act.activation(p_exp[:, :], p_exp[:, :], ACT.Exp).then_inc(p_exp_ready, 1)

            def step(b, par, r, prev=True, nxt=True):
                gate(b, par)
                hom_evac(b, par, 0)
                if prev:
                    turned_evac(b - 1)
                elu_exp(b, 0)
                if prev:
                    prob_exp(b - 1)
                hom_evac(b, par, 1)
                elu_exp(b, 1)
                if nxt:
                    project_evac(b + 1, 1 - par)
                second_norm(b, par, r)

            project_evac(0, 0)
            step(0, 0, 0, prev=False)
            step(1, 1, 0)
            step(2, 0, 1)
            with act.Fori(1, B // 2 - 1) as i:
                step(2 * i + 1, 1, i)
                step(2 * i + 2, 0, i + 1)
            step(B - 1, 1, B // 2 - 1, nxt=False)
            turned_evac(B - 1)
            prob_exp(B - 1)

            def tile_step(i, c):
                tau = R * i + c
                known = isinstance(tau, int)
                t = tau - 1
                if not known or t >= 0:
                    act.wait_ge(y_biased, t + 1)
                    act.activation(y_out[:, (c - 1) % R, :], y_b[:, (c + 1) % 2, :], ACT.Copy,
                                   scale=rt[:, (c - 1) % R, D + 1:D + 2]).then_inc(y_scaled, 1)
                t = tau + 2
                if not known or t < TILES:
                    act.wait_ge(rt_turned, t + 1)
                    act.activation(rt_t[:, c % 2, :], bank[c % 2][:, 0:P], ACT.Copy).then_inc(rt_t_ready, 1)
                t = tau + 1
                if not known or 0 <= t < TILES:
                    act.wait_ge(h_ready[0], t + 1)
                    for j in range(HC // 2):
                        m = act.activation(h_t[:, (c + 1) % 2, j * P:(j + 1) * P],
                                           bank[2 + 2 * ((c + 1) % 2)][:, j * P:(j + 1) * P], ACT.Relu,
                                           bias=w1[:, (c + 1) % W, H + j:H + j + 1])
                    m.then_inc(h_t_ready[0], 1)

            run_tiles(act, tile_step, -2)

            with act.Fori(0, B) as b:
                act.wait_ge(out_ready, b + 1)
                act.dma_start(out[bass.ds(b, 1), :, :].rearrange("b p n -> (b p) n"), x1[:, cols(b * TD, TD)]
                              ).then_inc(stored, 16)
            act.wait_ge(stored, 16 * B)

        @block.vector
        def _(dve):
            steps = [0]

            def fresh():
                dve.sem_clear(dve_chain)
                steps[0] = 0

            def link(ins):
                steps[0] += 1
                ins.then_inc(dve_chain, 1)
                dve.wait_ge(dve_chain, steps[0])

            def row_stats(b, par, ln, r=None):
                fresh()
                if ln == 0:
                    dve.wait_ge(x_loaded[par], 32 * (r + 1))
                else:
                    dve.wait_ge(x1_ready, 2 * (b + 1))
                dve.sem_inc(dve_waits, 1)
                for t in range(T):
                    last = dve.bn_stats(stats[:, ln, t, :], x1[:, cols(b * TD + t * D, D)])
                link(last)
                for t in range(T):
                    last = dve.bn_aggr(mean_var[:, ln, t, :], stats[:, ln, t, :])
                last.then_inc(stats_ready[ln], 1)

            def column_sums(b, par, r):
                dve.wait_ge(adj_loaded[par], 64 * (r + 1))
                if not isinstance(b, int) or b >= 1:
                    dve.wait_ge(deg_summed, b)
                dve.tensor_reduce(col_sum[:, :], adj_sb[:, par, :].rearrange("p (c n) -> p n c", c=T),
                                  AX_X, ALU.add).then_inc(sum_ready, 1)

            def gate_bias(b, par):
                dve.wait_ge(proj_read, T * (b + 1))
                g = het_gate[:, par, :, D:2 * D]
                dve.tensor_tensor(g, g, b_gate_sb[:, :].rearrange("p (o d) -> p o d", o=1).broadcast_to((P, T, D)),
                                  ALU.add).then_inc(gate_biased, 1)

            def degree(b):
                dve.wait_ge(deg_summed, b + 1)
                dve.tensor_scalar(deg_sb[:, :], deg_ps, DEG_EPS, None, ALU.add).then_inc(deg_read, 1)

            def combine(b, par, h):
                sl = slice(h * HALF, (h + 1) * HALF)
                het = het_gate[:, par, sl, 0:D]
                th = het_gate[:, par, sl, D:2 * D]
                z = z_sb[:, sl, :]
                fresh()
                dve.wait_ge(hom_read, 2 * b + h + 1)
                link(dve.tensor_tensor(z, z, het, ALU.subtract))
                dve.wait_ge(gate_ready, b + 1)
                link(dve.scalar_tensor_tensor(z, th, 1.0, z, ALU.add, ALU.mult))
                dve.scalar_tensor_tensor(z, z, 0.5, het, ALU.mult, ALU.add).then_inc(z_ready, 1)

            def residual(b, h):
                sl = slice(h * HALF, (h + 1) * HALF)
                z = z_sb[:, sl, :]
                xb = x1[:, cols(b * TD + h * HALF * D, HALF * D)]
                fresh()
                dve.wait_ge(exp_ready, 2 * b + h + 1)
                link(dve.scalar_tensor_tensor(z, z, 0.0, neg_sb[:, sl, :], ALU.max, ALU.add))
                dve.scalar_tensor_tensor(xb, z.rearrange("p t d -> p (t d)"), -1.0, xb, ALU.add, ALU.add
                                         ).then_inc(x1_ready, 1)

            def route(b, par):
                fresh()
                dve.wait_ge(gated, b + 1)
                dve.tensor_tensor(scores[:, :, :], gate_ps.rearrange("p (t e) -> p t e", t=T),
                                  b_router_sb[:, :].rearrange("p (o e) -> p o e", o=1).broadcast_to((P, T, NE)),
                                  ALU.add).then_inc(scores_ready, 1)
                dve.wait_ge(pool_const, 1)
                dve.wait_ge(scores_ready, b + 1)
                for t in range(T):
                    last = dve.max(top[:, t, :], scores[:, t, :])
                link(last)
                dve.tensor_tensor(p_exp[:, :], top[:, :, 1], top[:, :, 0], ALU.subtract).then_inc(gaps_ready, 1)
                for t in range(T):
                    last = dve.max_index(top_at[:, t, :], top[:, t, :], scores[:, t, :])
                link(last)
                link(dve.tensor_copy(top_f[:, :, :], top_at[:, :, 0:K].rearrange("p t k -> p k t")))
                iota4 = iota_e[:, :].rearrange("p (k t e) -> p k t e", k=1, t=1).broadcast_to((P, K, T, NE))
                top4 = top_f[:, :, :].rearrange("p k (t o) -> p k t o", o=1).broadcast_to((P, K, T, NE))
                link(dve.tensor_tensor(chosen[:, :, :, :], iota4, top4, ALU.is_equal))
                dve.tensor_tensor(picked[:, :, :], chosen[:, 0, :, :], chosen[:, 1, :, :], ALU.add
                                  ).then_inc(picked_ready, 1)
                if not isinstance(b, int) or b >= 2:
                    r = (b - par) // 2 if isinstance(b, int) else None
                    dve.wait_ge(scattered[par], 16 * K * T * (r if r is not None else route_r[0]))
                to = payload[:, par, :, :, D:D + 1].bitcast(I32)
                dve.tensor_scalar(to, to, float(2 * N), None, ALU.add)
                dve.wait_ge(p_exp_ready, b + 1)
                link(dve.tensor_scalar(p_sum[:, :], p_exp[:, :], 1.0, None, ALU.add))
                prob = [payload[:, par, k, :, D + 1] for k in range(K)]
                link(dve.reciprocal(prob[0], p_sum[:, :]))
                dve.tensor_tensor(prob[1], p_exp[:, :], prob[0], ALU.mult)

            def place_rows(b, par):
                fresh()
                dve.wait_ge(ranked, b + 1)
                nr = next_row[:, :].rearrange("p (o e) -> p o e", o=1).broadcast_to((P, T, NE))
                link(dve.tensor_tensor(place[:, :, :], rank_ps.rearrange("p (t e) -> p t e", t=T), nr, ALU.add))
                dve.tensor_tensor(next_row[:, :], next_row[:, :], total_ps, ALU.add)
                pl = place[:, :, :].rearrange("p (o t) e -> p o t e", o=1).broadcast_to((P, K, T, NE))
                link(dve.tensor_tensor(place_k[:, :, :, :], chosen[:, :, :, :], pl, ALU.mult))
                link(dve.tensor_reduce(slot_f[:, :, :], place_k[:, :, :, :], AX_X, ALU.add))
                dve.wait_ge(copied, b + 1)
                dve.tensor_copy(slot[:, par, :, :], slot_f[:, :, :]).then_inc(slots_ready, 1)

            route_r = [None]

            def step(b, par, r, prev=True, nxt=True):
                gate_bias(b, par)
                if nxt:
                    row_stats(b + 1, 1 - par, 0, r + par)
                    column_sums(b + 1, 1 - par, r + par)
                combine(b, par, 0)
                if prev:
                    route_r[0] = r - 1 + par
                    route(b - 1, 1 - par)
                residual(b, 0)
                if prev:
                    place_rows(b - 1, 1 - par)
                if nxt:
                    degree(b + 1)
                combine(b, par, 1)
                residual(b, 1)
                row_stats(b, par, 1)

            dve.wait_ge(pool_const, 1)
            dve.wait_ge(s_const, 64)
            dve.wait_ge(w_summed, 1)
            dve.scalar_tensor_tensor(w_gnn_sb[:, :], w_sum_ps, -1.0 / D, w_raw[:, :], ALU.mult, ALU.add
                                     ).then_inc(w_centred, 1)
            row_stats(0, 0, 0, 0)
            column_sums(0, 0, 0)
            degree(0)
            step(0, 0, 0, prev=False)
            step(1, 1, 0)
            step(2, 0, 1)
            with dve.Fori(1, B // 2 - 1) as i:
                step(2 * i + 1, 1, i)
                step(2 * i + 2, 0, i + 1)
            step(B - 1, 1, B // 2 - 1, nxt=False)
            route(B - 1, 1)
            place_rows(B - 1, 1)

            dve.wait_ge(slots_ready, B)
            dve.wait_ge(iotas, 1)
            dve.tensor_scalar(pad_slot, next_row[:, :], part_iota[:, 0:1], None, ALU.add).then_inc(pad_slots_ready, 1)
            fresh()
            for e in range(NE):
                last = dve.tensor_scalar(count_i[:, e:e + 1], next_row[:, e:e + 1], float(P - 1 - e * REG), None,
                                         ALU.add)
            link(last)
            link(dve.tensor_scalar(count_i[:, :], count_i[:, :], 7, None, ALU.logical_shift_right))
            link(dve.tensor_copy(tiles_e[:, :], count_i[:, :]))
            link(dve.tensor_copy(tiles_end[:, 0:1], tiles_e[:, 0:1]))
            for e in range(1, NE):
                link(dve.tensor_tensor(tiles_end[:, e:e + 1], tiles_end[:, e - 1:e], tiles_e[:, e:e + 1], ALU.add))
            link(dve.tensor_scalar(skip_e[:, :], tiles_e[:, :], -float(P), float(REG), ALU.mult, ALU.add))
            dve.tensor_scalar(tile_e[:, :], tile_iota, tiles_end[:, 0:1], None, ALU.is_ge)
            link(dve.tensor_scalar(tile_row[:, :], tile_iota, float(P), None, ALU.mult))
            for e in range(NE):
                if e:
                    dve.scalar_tensor_tensor(tile_e[:, :], tile_iota, tiles_end[:, e:e + 1], tile_e[:, :],
                                             ALU.is_ge, ALU.add)
                link(dve.tensor_scalar(reach[:, :], tile_iota, tiles_end[:, e:e + 1], skip_e[:, e:e + 1],
                                       ALU.is_ge, ALU.mult))
                link(dve.tensor_tensor(tile_row[:, :], tile_row[:, :], reach[:, :], ALU.add))
            link(dve.tensor_scalar(tile_e[:, :], tile_e[:, :], float(NE - 1), None, ALU.min))
            dve.tensor_scalar(tab_w2[:, :], tile_e[:, :], float(H), None, ALU.mult)
            dve.tensor_scalar(tab_e[:, :], tile_e[:, :], float(P), None, ALU.mult)
            dve.tensor_copy(tab_row[:, :], tile_row[:, :]).then_inc(tables_ready, 1)
            dve.wait_ge(tables_ready, 1)
            dve.wait_ge(s_bias, 16)

            def tile_step(i, c):
                tau = R * i + c
                known = isinstance(tau, int)
                t = tau - 1
                if not known or t >= 0:
                    s = (c - 1) % R
                    if not known or t >= R:
                        dve.wait_ge(returned[s], 16 * (i + (c - 1) // R))
                    dve.tensor_copy(dest[:, s:s + 1], rt[:, s, D:D + 1].bitcast(I32))
                    col = dve.value_load(tab_e[0:1, cols(t, 1)], min_val=0, max_val=(NE - 1) * D)
                    dve.wait_ge(y_ready, t + 1)
                    if not known or t >= 2:
                        dve.wait_ge(y_scaled, t - 1)
                    dve.tensor_tensor(y_b[:, (c + 1) % 2, :], bank[6 + (c + 1) % 2][:, 0:D],
                                      b2_sb[:, cols(col, D)], ALU.add).then_inc(y_biased, 1)
                t = tau + 1
                if not known or 0 <= t < TILES:
                    dve.wait_ge(h_ready[1], t + 1)
                    for j in range(HC // 2):
                        n = HC // 2 + j
                        m = dve.tensor_scalar(h_t[:, (c + 1) % 2, n * P:(n + 1) * P],
                                              bank[3 + 2 * ((c + 1) % 2)][:, j * P:(j + 1) * P],
                                              w1[:, (c + 1) % W, H + n:H + n + 1], 0.0, ALU.add, ALU.max)
                    m.then_inc(h_t_ready[1], 1)

            run_tiles(dve, tile_step, -1)

            with dve.Fori(0, B // 2) as r:
                for par in range(2):
                    b = 2 * r + par
                    fresh()
                    dve.wait_ge(y_loaded[par], 16 * K * (r + 1))
                    xb = x1[:, cols(b * TD, TD)]
                    link(dve.tensor_tensor(y_in[:, par, 0, :], y_in[:, par, 0, :], y_in[:, par, 1, :], ALU.add))
                    dve.tensor_tensor(xb, xb, y_in[:, par, 0, :], ALU.add).then_inc(out_ready, 1)


def kernel(x, adj, L0_gnn_W_t, L0_gnn_b_t, L0_gnn_W_h, L0_gnn_theta, L0_ffn_Wg, L0_ffn_bg, L0_ffn_W1, L0_ffn_b1,
           L0_ffn_W2, L0_ffn_b2):
    import numpy as np
    import concourse.bacc as bacc
    from concourse.bass_utils import run_bass_kernel_spmd as launch

    b, n, d = x.shape
    t = n // P
    ne, h, _ = L0_ffn_W1.shape
    c = np.ascontiguousarray
    rows = lambda a: c(np.broadcast_to(np.asarray(a).reshape(1, -1), (P, a.size)))
    adj_t = np.asarray(adj).reshape(b, P, t, P, t).transpose(0, 3, 4, 2, 1)
    w1_t = np.asarray(L0_ffn_W1).transpose(0, 2, 1)
    b1_t = np.asarray(L0_ffn_b1).reshape(ne, h // P, P).transpose(0, 2, 1)
    w2_t = np.asarray(L0_ffn_W2).reshape(ne, d, h // P, P).transpose(3, 0, 2, 1)
    arrays = {
        "x": c(np.asarray(x).reshape(b, P, t * d)),
        "x_t": c(np.asarray(x).reshape(b, P, t, d).transpose(0, 3, 2, 1)).reshape(b, d, n),
        "adj_t": c(adj_t).reshape(b, P, t * n),
        "w_gnn": c(np.concatenate([np.asarray(L0_gnn_theta), np.asarray(L0_gnn_W_h), np.asarray(L0_gnn_W_t)], 1)),
        "b_gate": rows(np.asarray(L0_gnn_b_t)),
        "wg_t": c(np.asarray(L0_ffn_Wg).T),
        "b_router": rows(np.asarray(L0_ffn_bg)),
        "w1b_t": c(np.concatenate([w1_t, b1_t], 2)).reshape(ne * d, h + h // P),
        "w2_t": c(w2_t).reshape(P, ne * h),
        "b2": rows(np.asarray(L0_ffn_b2)),
    }
    nc = bacc.Bacc("TRN2", target_bir_lowering=False, num_devices=1)
    args = [nc.dram_tensor(f"in_{k}", a.shape, F32, kind="ExternalInput").ap() for k, a in arrays.items()]
    out = nc.dram_tensor("out", (b, P, t * d), F32, kind="ExternalOutput").ap()
    build(nc, *args, out)
    got = launch(nc, [{f"in_{k}": a for k, a in arrays.items()}], core_ids=[0])
    return got.results[0]["out"].reshape(b, n, d)
```

```python
from contextlib import ExitStack

import concourse.bass as bass
from concourse import mybir

F32 = mybir.dt.float32
BF16 = mybir.dt.bfloat16
I32 = mybir.dt.int32
U32 = mybir.dt.uint32
ALU = mybir.AluOpType
ACT = mybir.ActivationFunctionType
AX_X = mybir.AxisListType.X

P = 128
EPS = 1e-5
DEG_EPS = 1e-6


def build(nc, x, x_t, adj_t, weights, b_gate, b_router, w1b_t, w2_t, b2, out):
    B, _, TD = x.shape
    D = P
    T = TD // D
    N = P * T
    NE = b_router.shape[1]
    H = w2_t.shape[1] // NE
    HC = H // P
    WB = H + HC
    K = 2
    TOK = B * N
    G = 2
    GB = [B - B // 2 + 1, B // 2 - 1]
    B0 = GB[0]
    first_batch = [0, B0, B]
    REG = TOK + P
    GROWS = NE * REG
    SPARE = NE
    GT = [K * N * n // P + SPARE for n in GB]
    first_tile = [0, GT[0], GT[0] + GT[1]]
    TILES = first_tile[G]
    ROW = D + 2
    GN = 3 * D
    R = 8
    TURNS = TILES // R
    TURN1 = GT[0] // R
    C_TURN = TURNS - B0
    HALF = T // 2
    QT = 4

    routed = nc.dram_tensor("routed", (G * GROWS + SPARE * P, ROW), F32, kind="Internal").ap()
    expert_out = nc.dram_tensor("expert_out", (K * TOK + (G * NE + SPARE) * P, D), F32, kind="Internal").ap()
    expert_out_kb = expert_out[0:K * TOK, :].rearrange("(k b p t) d -> k b p (t d)", k=K, b=B, p=P)

    with ExitStack() as ctx:
        def sb(name, shape, dt=F32):
            return ctx.enter_context(nc.sbuf_tensor(name, shape, dt))

        def ps(name, shape):
            return ctx.enter_context(nc.psum_tensor(name, shape, F32))

        def sem(name):
            return ctx.enter_context(nc.semaphore(name))

        w_raw = sb("w_raw", [P, GN + NE])
        w_centred_sb = sb("w_centred_sb", [P, GN + NE])
        w_gnn_sb, wg_sb = w_centred_sb[:, 0:GN], w_centred_sb[:, GN:GN + NE]
        b_gate_sb = sb("b_gate_sb", [P, D])
        b_router_sb = sb("b_router_sb", [P, NE])
        w2_sb = sb("w2_sb", [P, NE * H])
        ident = sb("ident", [P, P])
        ones_f = sb("ones_f", [P, P])
        before = sb("before", [P, P], BF16)
        ones_bf = sb("ones_bf", [P, P], BF16)
        iota_e = sb("iota_e", [P, NE])
        minus_half = sb("minus_half", [P, T])

        adj_sb = sb("adj_sb", [P, 2, T * N])
        x1 = sb("x1", [P, B * TD])
        x_t_sb = sb("x_t_sb", [P, 2, N])
        f_hom = sb("f_hom", [P, T, D])
        het_gate = sb("het_gate", [P, 2, T, 2 * D])
        col_sum = sb("col_sum", [P, N])
        x1_t = sb("x1_t", [P, N])
        z_sb = sb("z_sb", [P, 2, T, D])
        neg_sb = sb("neg_sb", [P, T, D])
        neg_mean = sb("neg_mean", [P, T])
        squares = sb("squares", [P, T])
        unused = sb("unused", [P, T, D])
        var_eps = sb("var_eps", [P, T])
        deg_sb = sb("deg_sb", [P, T])
        norm_rstd = sb("norm_rstd", [P, 2, 2, T])
        norm_x_rstd = sb("norm_x_rstd", [P, 2, T])
        stats = sb("stats", [P, T, 6])
        mean_var = sb("mean_var", [P, T, 2])
        rstd = sb("rstd", [P, T])
        shift = sb("shift", [P, T])
        payload = sb("payload", [P, 2, K, T, ROW])
        scores = sb("scores", [P, T, NE])
        top = sb("top", [P, T, 8])
        top_at = sb("top_at", [P, T, 8], U32)
        top_f = sb("top_f", [P, K, T])
        chosen = sb("chosen", [P, K, T, NE])
        picked = sb("picked", [P, T, NE], BF16)
        place = sb("place", [P, T, NE])
        place_k = sb("place_k", [P, K, T, NE])
        slot_f = sb("slot_f", [P, K, T])
        slot = sb("slot", [P, 2, K, T], I32)
        next_row = sb("next_row", [P, (B + 1) * NE])
        group_at = sb("group_at", [P, B])
        pad_rows = sb("pad_rows", [P, NE, ROW])
        p_exp = sb("p_exp", [P, T])
        p_sum = sb("p_sum", [P, T])

        used = [0, 0]

        def in_adj(buf, n):
            at = used[buf]
            used[buf] += n
            assert used[buf] <= T * N
            return adj_sb[:, buf, at:at + n]

        b2_sb = in_adj(1, NE * D)
        y_in = in_adj(1, 3 * K * TD).rearrange("p (s k n) -> p s k n", s=3, k=K)
        rt = in_adj(0, R * ROW).rearrange("p (s r) -> p s r", r=ROW)
        w1 = in_adj(0, R * WB).rearrange("p (s n) -> p s n", s=R)
        rt_t = in_adj(0, 2 * P).rearrange("p (s n) -> p s n", s=2)
        h_t = in_adj(0, 2 * H).rearrange("p (s n) -> p s n", s=2)
        y_b = in_adj(0, 2 * D).rearrange("p (s n) -> p s n", s=2)
        y_out = in_adj(0, R * D).rearrange("p (s n) -> p s n", s=R)
        dest = in_adj(0, R).bitcast(I32)
        pad_at = sb("pad_at", [P, G, NE], I32)
        tile_iota = sb("tile_iota", [P, max(GT)])
        upto = sb("upto", [P, NE, NE])
        count_i = sb("count_i", [P, NE], I32)
        tiles_e = sb("tiles_e", [P, NE])
        tiles_upto = sb("tiles_upto", [P, NE, NE])
        tiles_end = sb("tiles_end", [P, NE])
        row_of = sb("row_of", [P, NE + 1])
        row_step = sb("row_step", [P, NE])
        reach = sb("reach", [P, max(GT), NE])
        tile_e = sb("tile_e", [P, max(GT)])
        tile_row = sb("tile_row", [P, max(GT)])
        tab_w2 = sb("tab_w2", [P, TILES], I32)
        tab_e = sb("tab_e", [P, TILES], I32)
        tab_row = sb("tab_row", [P, TILES], I32)

        bank = [ps(f"bank{i}", [P, 512]) for i in range(8)]
        hom_ps = bank[0:2]
        turn_ps = bank[2:4]
        proj_ps = bank[4:6]
        w_sum_ps = bank[7][:, 0:GN + NE]
        gate_ps = bank[6][:, 0:T * NE]
        deg_ps = bank[4][:, GN:GN + T]
        deg_0_ps = bank[6][:, 128:128 + T]
        rank_ps, total_ps = bank[7][:, 0:T * NE], bank[7][:, 128:128 + NE]

        s_const = sem("s_const")
        s_wexp = sem("s_wexp")
        s_bias = sem("s_bias")
        x_loaded = [sem(f"x_loaded{i}") for i in range(2)]
        x_t_loaded = [sem(f"x_t_loaded{i}") for i in range(2)]
        adj_loaded = [[sem(f"adj_loaded{i}_{q}") for q in range(QT)] for i in range(2)]
        adj_used = sem("adj_used")
        pool_const = sem("pool_const")
        means_ready, squares_ready = sem("means_ready"), sem("squares_ready")
        rstd_0_ready, f_hom_ready = sem("rstd_0_ready"), sem("f_hom_ready")
        stats_ready, rstd_ready = sem("stats_ready"), sem("rstd_ready")
        w_summed, w_centred = sem("w_summed"), sem("w_centred")
        turned, x1_t_ready = sem("turned"), sem("x1_t_ready")
        sum_parts = sem("sum_parts")
        deg_summed, deg_read, norm_ready = sem("deg_summed"), sem("deg_read"), sem("norm_ready")
        projected, proj_read = sem("projected"), sem("proj_read")
        gate_biased, gate_ready = sem("gate_biased"), sem("gate_ready")
        hom_ready, hom_read = sem("hom_ready"), sem("hom_read")
        x1_ready = sem("x1_ready")
        z_ready, z_negated, exp_ready = sem("z_ready"), sem("z_negated"), sem("exp_ready")
        x2n_ready = sem("x2n_ready")
        gated, scores_ready, gaps_ready = sem("gated"), sem("scores_ready"), sem("gaps_ready")
        x1_kept = sem("x1_kept")
        picked_ready, ranked = sem("picked_ready"), sem("ranked")
        p_exp_ready = sem("p_exp_ready")
        slots_ready, shift_ready, copied = sem("slots_ready"), sem("shift_ready"), sem("copied")
        scattered = [sem(f"scattered{i}") for i in range(2)]
        dve_chain, pool_chain = sem("dve_chain"), sem("pool_chain")
        dve_waits, pool_waits, act_waits = sem("dve_waits"), sem("pool_waits"), sem("act_waits")
        spares_ready, spares_written = sem("spares_ready"), sem("spares_written")
        pads_ready, pads_written = sem("pads_ready"), sem("pads_written")
        pad_at_ready, tables_ready = sem("pad_at_ready"), sem("tables_ready")
        rt_loaded = [sem(f"rt_loaded{i}") for i in range(R)]
        w1_loaded = [sem(f"w1_loaded{i}") for i in range(R)]
        rt_turned, rt_t_ready = sem("rt_turned"), sem("rt_t_ready")
        h_ready = [sem("h_ready_act"), sem("h_ready_dve")]
        h_t_ready = [sem("h_t_ready_act"), sem("h_t_ready_dve")]
        y_ready, y_biased, y_scaled = sem("y_ready"), sem("y_biased"), sem("y_scaled")
        returned = [sem(f"returned{i}") for i in range(R)]
        y_loaded = [sem(f"y_loaded{i}") for i in range(2)]
        y_last_loaded = [sem(f"y_last_loaded{h}") for h in range(2)]
        out_ready = sem("out_ready")
        stored = sem("stored")

        assert P == D, "a tile's table entry tab_e serves rows of w1b_t and columns of b2_sb"
        block = ctx.enter_context(nc.Block())

        def run_tiles(eng, tile_step, first, beside, cuts=(), between=None):
            for c in range(R + first, R):
                tile_step(-1, c)
            for c in range(R + 1):
                tile_step(0, c)
                beside(c)
            ends = [1, *cuts, TURNS - 1]
            for a, z in zip(ends, ends[1:]):
                if a > 1:
                    between(a)
                with eng.Fori(a, z) as i:
                    for c in range(1, R + 1):
                        tile_step(i, c)
            for c in range(1, R + 1):
                tile_step(TURNS - 1, c)

        QTR = T * N // QT

        def cols(at, n):
            return bass.ds(at, n)

        @block.sync
        def _(sp):
            def load_rows(b, par):
                sp.dma_start(x1[:, cols(b * TD, TD)], x[bass.ds(b, 1), :, :].rearrange("b p n -> (b p) n")
                             ).then_inc(x_loaded[par], 16)

            def load_turned(b, par):
                if not isinstance(b, int) or b >= 2:
                    sp.wait_ge(projected, T * (b - 1))
                sp.dma_start(x_t_sb[:, par, :], x_t[bass.ds(b, 1), :, :].rearrange("b p n -> (b p) n")
                             ).then_inc(x_t_loaded[par], 16)

            def load_adj(b, par):
                for q in range(QT):
                    if not isinstance(b, int) or b >= 2:
                        sp.wait_ge(adj_used, QT * (b - 2) + q + 1)
                    sp.dma_start(adj_sb[:, par, q * QTR:(q + 1) * QTR],
                                 adj_t[bass.ds(b, 1), :, q * QTR:(q + 1) * QTR].rearrange("b p n -> (b p) n")
                                 ).then_inc(adj_loaded[par][q], 16)

            load_rows(0, 0)
            for dst, src in ((w_raw, weights), (b_gate_sb, b_gate), (b_router_sb, b_router)):
                sp.dma_start(dst[:, :], src).then_inc(s_const, 16)
            load_turned(0, 0)
            load_adj(0, 0)
            load_rows(1, 1)
            load_adj(1, 1)
            load_turned(1, 1)
            sp.dma_start(w2_sb[:, :], w2_t).then_inc(s_wexp, 16)
            sp.wait_ge(spares_ready, 1)
            for j in range(SPARE):
                sp.dma_start(routed[G * GROWS + j * P:G * GROWS + (j + 1) * P, :], pad_rows[:, j, :]
                             ).then_inc(spares_written, 16)
            with sp.Fori(1, B // 2) as r:
                for par in range(2):
                    load_turned(2 * r + par, par)
                    load_rows(2 * r + par, par)
                    load_adj(2 * r + par, par)

            def entries(tab, at, n, most):
                return nc.values_load_multi_w_load_instructions(
                    tab[0:1, cols(at, n)], engines=(mybir.EngineType.SP,), min_val=0, max_val=most,
                    skip_runtime_bounds_check_because="the table's entries lie in these bounds for any routing"
                )[1]

            def write_pads(g):
                sp.wait_ge(pads_ready, g + 1)
                sp.wait_ge(pad_at_ready, g + 1)
                ends = entries(pad_at[:, g, :], 0, NE, G * GROWS - P)
                for e in range(NE):
                    sp.dma_start(routed[bass.ds(ends[e], P), :], pad_rows[:, e, :]).then_inc(pads_written, 16)

            def load_turn(i):
                rows = entries(tab_row, R * i, R, G * GROWS + (SPARE - 1) * P)
                experts = entries(tab_e, R * i, R, (NE - 1) * P)
                for s in range(R):
                    if not isinstance(i, int) or i >= 1:
                        sp.wait_ge(y_scaled, R * (i - 1) + s + 1)
                    sp.dma_start(rt[:, s, :], routed[bass.ds(rows[s], P), :]).then_inc(rt_loaded[s], 16)
                    sp.dma_start(w1[:, s, :], w1b_t[bass.ds(experts[s], P), :]).then_inc(w1_loaded[s], 16)

            def group_routed(g):
                sp.wait_ge(tables_ready, g + 1)
                n = first_batch[g + 1]
                sp.wait_ge(scattered[0], 16 * K * T * ((n + 1) // 2))
                sp.wait_ge(scattered[1], 16 * K * T * (n // 2))
                sp.wait_ge(pads_written, 16 * NE * (g + 1))

            def load_y(b, par):
                if not isinstance(b, int) or b >= 2:
                    sp.wait_ge(out_ready, b - 1)
                for k in range(K):
                    sp.dma_start(y_in[:, par, k, :],
                                 expert_out_kb[k, bass.ds(b, 1), :, :].rearrange("b p n -> (b p) n")
                                 ).then_inc(y_loaded[par], 16)

            write_pads(0)
            group_routed(0)
            sp.wait_ge(spares_written, 16 * SPARE)
            sp.wait_ge(hom_ready, 2 * (B - 1))
            load_turn(0)
            sp.wait_ge(hom_ready, 2 * B)
            sp.dma_start(b2_sb, b2).then_inc(s_bias, 16)
            with sp.Fori(1, TURN1 - 2) as i:
                load_turn(i)
            write_pads(1)
            with sp.Fori(TURN1 - 2, TURN1) as i:
                load_turn(i)
            group_routed(1)
            with sp.Fori(TURN1, C_TURN) as i:
                load_turn(i)
            for s in range(R):
                sp.wait_ge(returned[s], 16 * TURN1)
            for b in range(2):
                load_y(b, b)
                load_turn(C_TURN + b)
            with sp.Fori(1, B0 // 2) as r:
                for par in range(2):
                    load_y(2 * r + par, par)
                    load_turn(C_TURN + 2 * r + par)
            load_y(B0 - 1, 0)
            load_turn(TURNS - 1)
            for s in range(R):
                sp.wait_ge(returned[s], 16 * TURNS)
            for b in range(B0, B - 1):
                load_y(b, b % 2)
            for h in range(2):
                half = slice(h * TD // 2, (h + 1) * TD // 2)
                for k in range(K):
                    sp.dma_start(y_in[:, 2, k, half], expert_out_kb[k, B - 1, :, half]).then_inc(y_last_loaded[h], 16)

        @block.gpsimd
        def _(pool):
            pool.memset(ident[:, :], 0.0).then_inc(pool_chain, 1)
            pool.memset(ones_bf[:, :], 1.0).then_inc(pool_chain, 1)
            pool.memset(ones_f[:, :], 1.0)
            pool.memset(minus_half[:, :], -0.5)
            pool.wait_ge(pool_chain, 2)
            pool.affine_select(out=ident[:, :], in_=ident[:, :], compare_op=ALU.not_equal, fill=1.0, base=0,
                               pattern=[[-1, P]], channel_multiplier=1)
            pool.affine_select(out=before[:, :], in_=ones_bf[:, :], compare_op=ALU.is_gt, fill=0.0, base=0,
                               pattern=[[1, P]], channel_multiplier=-1)
            pool.iota(iota_e[:, :], pattern=[[1, NE]], base=0, channel_multiplier=0,
                      allow_small_or_imprecise_dtypes=True)
            pool.iota(next_row[:, 0:NE], pattern=[[REG, NE]], base=0, channel_multiplier=0,
                      allow_small_or_imprecise_dtypes=True)
            pool.iota(tile_iota[:, :], pattern=[[1, max(GT)]], base=0, channel_multiplier=0,
                      allow_small_or_imprecise_dtypes=True)
            for g in range(G):
                pool.memset(group_at[:, first_batch[g]:first_batch[g + 1]], float(g * GROWS))
            pool.memset(pad_rows[:, :, :], 0.0).then_inc(pool_chain, 1)
            pool.memset(upto[:, :, :], 0.0).then_inc(pool_chain, 1)
            pool.wait_ge(pool_chain, 4)
            for e in range(NE):
                pool.memset(upto[:, e, 0:e + 1], 1.0)
            pool.iota(pad_rows[:, :, D:D + 1].bitcast(I32), pattern=[[P, NE], [0, 1]], base=K * TOK + G * NE * P,
                      channel_multiplier=1).then_inc(spares_ready, 1)
            for par in range(2):
                last = pool.iota(payload[:, par, :, :, D:D + 1].bitcast(I32), pattern=[[TOK, K], [1, T], [0, 1]], base=(par - 2) * N,
                                 channel_multiplier=T)
            last.then_inc(pool_const, 1)

            def held():
                pool.sem_inc(pool_waits, 1)

            def first_norm(b, par):
                pool.sem_clear(pool_chain)
                pool.wait_ge(deg_read, b + 1)
                pool.tensor_tensor(norm_rstd[:, par, 0, :], deg_sb[:, :], minus_half[:, :], ALU.pow
                                   ).then_inc(pool_chain, 1)
                pool.wait_ge(squares_ready, b + 1)
                held()
                pool.tensor_scalar(var_eps[:, :], squares[:, :], 1.0 / D, EPS, ALU.mult, ALU.add
                                   ).then_inc(pool_chain, 1)
                pool.wait_ge(pool_chain, 2)
                pool.tensor_tensor(norm_rstd[:, par, 1, :], var_eps[:, :], minus_half[:, :], ALU.pow
                                   ).then_inc(pool_chain, 1)
                pool.wait_ge(pool_chain, 3)
                pool.tensor_tensor(norm_x_rstd[:, par, :], norm_rstd[:, par, 0, :], norm_rstd[:, par, 1, :], ALU.mult
                                   ).then_inc(norm_ready, 1)

            def second_rstd(b):
                pool.sem_clear(pool_chain)
                pool.wait_ge(stats_ready, b + 1)
                held()
                pool.tensor_scalar(rstd[:, :], mean_var[:, :, 1], EPS, None, ALU.add).then_inc(pool_chain, 1)
                pool.wait_ge(pool_chain, 1)
                pool.tensor_tensor(rstd[:, :], rstd[:, :], minus_half[:, :], ALU.pow).then_inc(rstd_ready, 1)

            def second_shift(b):
                pool.sem_clear(pool_chain)
                pool.wait_ge(rstd_ready, b + 1)
                pool.tensor_tensor(shift[:, :], mean_var[:, :, 0], rstd[:, :], ALU.mult
                                   ).then_inc(pool_chain, 1)
                pool.wait_ge(pool_chain, 1)
                pool.tensor_scalar(shift[:, :], shift[:, :], -1.0, None, ALU.mult).then_inc(shift_ready, 1)

            def scatter(b, par, which, first=False):
                if first:
                    pool.wait_ge(copied, b + 1)
                    pool.wait_ge(slots_ready, b + 1)
                    held()
                for n in which:
                    k, t = n // T, n % T
                    pool.indirect_dma_start(
                        routed[:, :], bass.IndirectOffsetOnAxis(ap=slot[:, par, k, t:t + 1], axis=0),
                        payload[:, par, k, t, :], None).then_inc(scattered[par], 16)

            def pad_ids(g):
                if g == 0:
                    pool.wait_ge(spares_written, 16 * SPARE)
                else:
                    pool.wait_ge(pads_written, 16 * NE * g)
                pool.iota(pad_rows[:, :, D:D + 1].bitcast(I32), pattern=[[P, NE], [0, 1]],
                          base=K * TOK + g * NE * P, channel_multiplier=1).then_inc(pads_ready, 1)

            def step(b, par, prev=2, nxt=True):
                if prev > 1:
                    scatter(b - 2, par, range(0, 3), first=True)
                if prev:
                    second_rstd(b - 1)
                    second_shift(b - 1)
                if prev > 1:
                    scatter(b - 2, par, range(3, 6))
                if nxt:
                    first_norm(b + 1, 1 - par)
                if prev > 1:
                    scatter(b - 2, par, range(6, K * T))

            pool.sem_clear(pool_chain)
            pool.wait_ge(squares_ready, 1)
            pool.tensor_scalar(var_eps[:, :], squares[:, :], 1.0 / D, EPS, ALU.mult, ALU.add).then_inc(pool_chain, 1)
            pool.wait_ge(pool_chain, 1)
            pool.tensor_tensor(norm_rstd[:, 0, 1, :], var_eps[:, :], minus_half[:, :], ALU.pow
                               ).then_inc(rstd_0_ready, 1)
            pool.wait_ge(deg_read, 1)
            pool.tensor_tensor(norm_rstd[:, 0, 0, :], deg_sb[:, :], minus_half[:, :], ALU.pow
                               ).then_inc(norm_ready, 1)
            step(0, 0, prev=0)
            step(1, 1, prev=1)
            step(2, 0)
            pad_ids(0)
            with pool.Fori(1, B // 2 - 1) as i:
                step(2 * i + 1, 1)
                step(2 * i + 2, 0)
            step(B - 1, 1, nxt=False)
            second_rstd(B - 1)
            second_shift(B - 1)

            def send(t, s):
                pool.wait_ge(y_scaled, t + 1)
                held()
                pool.indirect_dma_start(
                    expert_out[:, :], bass.IndirectOffsetOnAxis(ap=dest[:, s:s + 1], axis=0),
                    y_out[:, s, :], None).then_inc(returned[s], 16)

            def late(n):
                b = B - 2 + n // (K * T)
                scatter(b, b % 2, range(n % (K * T), n % (K * T) + 1), first=(n % (K * T) == 0))

            LATE_TURNS = TURN1 - 3
            every = LATE_TURNS * R // (2 * K * T)
            pad_ids(1)
            for t in range(LATE_TURNS * R):
                send(t, t % R)
                if (t + 1) % every == 0 and t // every < 2 * K * T:
                    late(t // every)
            with pool.Fori(LATE_TURNS, TURNS) as i:
                for s in range(R):
                    send(R * i + s, s)

        @block.tensor
        def _(pe):
            def turn_x1(b, par, to=turn_ps):
                for h in range(2):
                    pe.wait_ge(x1_ready, 2 * b + h + 1)
                    for j in range(HALF):
                        m = pe.transpose(to[h][:, j * P:(j + 1) * P], z_sb[:, par, h * HALF + j, :], ident[:, :])
                    m.then_inc(turned, 1)

            def router(b):
                pe.wait_ge(x1_t_ready, 2 * (b + 1))
                for t in range(T):
                    m = pe.matmul(gate_ps[:, t * NE:(t + 1) * NE], x1_t[:, t * P:(t + 1) * P], wg_sb,
                                  start=True, stop=True)
                m.then_inc(gated, 1)

            def ranks(b):
                pe.wait_ge(picked_ready, b + 1)
                flat = picked[:, :, :].rearrange("p t e -> p (t e)")
                pe.matmul(rank_ps, before[:, :], flat, start=True, stop=False, skip_group_check=True)
                for s in range(1, T):
                    pe.matmul(rank_ps[:, s * NE:], ones_bf[:, :], flat[:, 0:(T - s) * NE], start=False,
                              stop=(s == T - 1), skip_group_check=True)
                for t in range(T):
                    m = pe.matmul(total_ps, ones_bf[:, :], picked[:, t, :], start=(t == 0), stop=(t == T - 1),
                                  skip_group_check=True)
                m.then_inc(ranked, 1)

            def degree(b, ps=deg_ps):
                pe.wait_ge(sum_parts, QT * (b + 1))
                for t in range(T):
                    m = pe.matmul(ps[:, t:t + 1], col_sum[:, t * P:(t + 1) * P], ones_f[:, 0:1],
                                  start=True, stop=True)
                m.then_inc(deg_summed, 1)

            def project(b, par, r, tiles):
                if tiles[0] == 0:
                    pe.wait_ge(x_t_loaded[par], 16 * (r + 1))
                    if not isinstance(b, int) or b >= 1:
                        pe.wait_ge(deg_read, b + 1)
                for t in tiles:
                    if not isinstance(b, int) or b * T + t >= 2:
                        pe.wait_ge(proj_read, T * b + t - 1)
                    pe.matmul(proj_ps[t % 2][:, 0:GN], x_t_sb[:, par, t * P:(t + 1) * P], w_gnn_sb,
                              start=True, stop=True).then_inc(projected, 1)

            def aggregate(b, par, h, blocks):
                for c in blocks:
                    if h == 0:
                        pe.wait_ge(proj_read, T * b + c + 1)
                        if isinstance(b, int) and b == 0:
                            pe.wait_ge(f_hom_ready, 1 + c // HALF)
                    if c == 0 and (not isinstance(b, int) or b >= 1):
                        pe.wait_ge(hom_read, 2 * (b - 1) + h + 1)
                    for j in range(HALF):
                        at = (c * T + h * HALF + j) * P
                        m = pe.matmul(hom_ps[h][:, j * P:(j + 1) * P], adj_sb[:, par, at:at + P],
                                      f_hom[:, c, :], start=(c == 0 and j == 0), stop=(c == T - 1),
                                      skip_group_check=True)
                    if h == 1 and c % 2 == 1:
                        m.then_inc(adj_used, 1)
                    if c == T - 1 and h == 0:
                        m.then_inc(hom_ready, 1)
                    if c == T - 1 and h == 1:
                        pe.wait_ge(adj_used, QT * (b + 1))
                        pe.sem_inc(hom_ready, 1)

            def step(b, par, r, prev=True, nxt=True):
                aggregate(b, par, 0, range(0, 6))
                if prev:
                    turn_x1(b - 1, 1 - par)
                aggregate(b, par, 0, range(6, T))
                if prev:
                    router(b - 1)
                aggregate(b, par, 1, range(0, 2))
                if nxt:
                    degree(b + 1)
                aggregate(b, par, 1, range(2, 4))
                for c in range(3, T):
                    if c > 3:
                        aggregate(b, par, 1, range(c, c + 1))
                    if nxt:
                        project(b + 1, 1 - par, r + par, range(c - 3, c - 2))
                    if c == (4 if nxt else 6) and prev:
                        ranks(b - 1)
                if nxt:
                    project(b + 1, 1 - par, r + par, range(5, T))

            pe.wait_ge(pool_const, 1)
            pe.wait_ge(s_const, 48)
            pe.matmul(w_sum_ps, ones_f[:, :], w_raw[:, :], start=True, stop=True).then_inc(w_summed, 1)
            pe.wait_ge(w_centred, 1)
            project(0, 0, 0, range(T))
            degree(0, deg_0_ps)
            step(0, 0, 0, prev=False)
            step(1, 1, 0)
            step(2, 0, 1)
            with pe.Fori(1, B // 2 - 1) as i:
                step(2 * i + 1, 1, i)
                step(2 * i + 2, 0, i + 1)
            step(B - 1, 1, B // 2 - 1, nxt=False)

            def last_router_read(t):
                if t == 2:
                    pe.wait_ge(x1_t_ready, 2 * B)
                if t == 4:
                    pe.wait_ge(scores_ready, B)
                if t == 7:
                    pe.wait_ge(slots_ready, B)

            def tile_step(i, c):
                tau = R * i + c
                known = isinstance(tau, int)
                if not known or tau >= 1:
                    col = pe.value_load(tab_w2[0:1, cols(tau - 1, 1)], min_val=0, max_val=(NE - 1) * H)
                t = tau + 2
                if not known or t < TILES:
                    s = (c + 2) % R
                    pe.wait_ge(rt_loaded[s], 16 * (i + (c + 2) // R + 1))
                    pe.transpose(bank[4 + c % 2][:, 0:P], rt[:, s, 0:D], ident[:, :]).then_inc(rt_turned, 1)
                t = tau - 1
                if not known or t >= 0:
                    for half in range(2):
                        pe.wait_ge(h_t_ready[half], t + 1)
                    if not known or t >= 2:
                        pe.wait_ge(y_biased, t - 1)
                    if known:
                        last_router_read(t)
                    for j in range(HC):
                        m = pe.matmul(bank[6 + (c + 1) % 2][:, 0:D], h_t[:, (c + 1) % 2, j * P:(j + 1) * P],
                                      w2_sb[:, cols(col + j * D, D)], start=(j == 0), stop=(j == HC - 1))
                    m.then_inc(y_ready, 1)
                t = tau + 1
                if not known or 0 <= t < TILES:
                    if known and t == 0:
                        pe.wait_ge(hom_read, 2 * B)
                    pe.wait_ge(w1_loaded[(c + 1) % R], 16 * (i + (c + 1) // R + 1))
                    pe.wait_ge(rt_t_ready, t + 1)
                    for half in range(2):
                        for j in range(HC // 2):
                            n = half * HC // 2 + j
                            m = pe.matmul(bank[2 * ((c + 1) % 2) + half][:, j * P:(j + 1) * P],
                                          w1[:, (c + 1) % R, n * P:(n + 1) * P], rt_t[:, (c + 1) % 2, :],
                                          start=True, stop=True)
                        m.then_inc(h_ready[half], 1)

            pe.wait_ge(tables_ready, 1)
            pe.wait_ge(s_wexp, 16)
            def beside(c):
                if c == 2:
                    pe.wait_ge(slots_ready, B - 1)
                    pe.wait_ge(y_biased, 2)
                    turn_x1(B - 1, 1, bank[6:8])
                if c == 3:
                    pe.wait_ge(y_biased, 3)
                    router(B - 1)
                if c == 6:
                    pe.wait_ge(y_biased, 6)
                    ranks(B - 1)

            run_tiles(pe, tile_step, -2, beside, (TURN1,), lambda i: pe.wait_ge(tables_ready, 2))

        @block.scalar
        def _(act):
            def turned_evac(b, ps=turn_ps):
                for h in range(2):
                    act.wait_ge(turned, 2 * b + h + 1)
                    act.activation(x1_t[:, h * HALF * P:(h + 1) * HALF * P], ps[h][:, :], ACT.Copy
                                   ).then_inc(x1_t_ready, 1)

            def row_means(b, par, r, tiles):
                if tiles[0] == 0:
                    act.wait_ge(x_loaded[par], 16 * (r + 1))
                    if not isinstance(b, int) or b >= 1:
                        act.wait_ge(norm_ready, b)
                    act.sem_inc(act_waits, 1)
                for t in tiles:
                    m = act.activation(unused[:, t, :], x1[:, cols(b * TD + t * D, D)], ACT.Copy, scale=-1.0 / D,
                                       accum_out=neg_mean[:, t:t + 1])
                if tiles[-1] == T - 1:
                    m.then_inc(means_ready, 1)

            def row_squares(b):
                act.wait_ge(means_ready, b + 1)
                act.sem_inc(act_waits, 1)
                for t in range(T):
                    m = act.activation(unused[:, t, :], x1[:, cols(b * TD + t * D, D)], ACT.Square,
                                       bias=neg_mean[:, t:t + 1], accum_out=squares[:, t:t + 1])
                m.then_inc(squares_ready, 1)

            def project_evac(b, par, tiles):
                early = isinstance(b, int) and b == 0
                if early:
                    act.wait_ge(rstd_0_ready, 1)
                elif tiles[0] == 0:
                    act.wait_ge(norm_ready, b + 1)
                for t in tiles:
                    act.wait_ge(projected, T * b + t + 1)
                    act.activation(f_hom[:, t, :], proj_ps[t % 2][:, 0:D], ACT.Copy,
                                   scale=norm_rstd[:, 0, 1, t:t + 1] if early else norm_x_rstd[:, par, t:t + 1])
                    act.activation(het_gate[:, par, t, :], proj_ps[t % 2][:, D:GN], ACT.Copy,
                                   scale=norm_rstd[:, par, 1, t:t + 1]).then_inc(proj_read, 1)

            def hom_evac(b, par, h):
                act.wait_ge(hom_ready, 2 * b + h + 1)
                if h == 0:
                    if not isinstance(b, int) or b >= 2:
                        act.wait_ge(turned, 2 * (b - 1))
                        act.wait_ge(x1_kept, b - 1)
                for j in range(HALF):
                    t = h * HALF + j
                    m = act.activation(z_sb[:, par, t, :], hom_ps[h][:, j * P:(j + 1) * P], ACT.Copy,
                                       scale=norm_rstd[:, par, 0, t:t + 1])
                m.then_inc(hom_read, 1)

            def second_norm(b, par, r, tiles):
                if tiles[0] == 0:
                    act.wait_ge(shift_ready, b + 1)
                    if not isinstance(b, int) or b >= 2:
                        act.wait_ge(scattered[par], 16 * K * T * r)
                for t in tiles:
                    m = act.activation(payload[:, par, 0, t, 0:D], z_sb[:, par, t, :], ACT.Identity,
                                       bias=shift[:, t:t + 1], scale=rstd[:, t:t + 1])
                if tiles[-1] == T - 1:
                    m.then_inc(x2n_ready, 1)

            def copy_rows(b, par):
                act.wait_ge(x2n_ready, b + 1)
                act.activation(payload[:, par, 1, :, 0:D], payload[:, par, 0, :, 0:D], ACT.Copy
                               ).then_inc(copied, 1)

            def keep(b, par):
                act.activation(x1[:, cols(b * TD, TD)], z_sb[:, par, :, :].rearrange("p t d -> p (t d)"), ACT.Copy
                               ).then_inc(x1_kept, 1)

            def gate(b, par):
                act.wait_ge(gate_biased, b + 1)
                g = het_gate[:, par, :, D:2 * D]
                act.activation(g, g, ACT.Tanh, scale=0.5).then_inc(gate_ready, 1)

            def elu_exp(b, par, h):
                sl = slice(h * HALF, (h + 1) * HALF)
                act.wait_ge(z_ready, 2 * b + h + 1)
                act.activation(neg_sb[:, sl, :], z_sb[:, par, sl, :], ACT.Relu, scale=-1.0).then_inc(z_negated, 1)
                act.wait_ge(z_negated, 2 * b + h + 1)
                act.activation(neg_sb[:, sl, :], neg_sb[:, sl, :], ACT.Exp, scale=-1.0).then_inc(exp_ready, 1)

            def prob_exp(b):
                act.wait_ge(gaps_ready, b + 1)
                act.activation(p_exp[:, :], p_exp[:, :], ACT.Exp).then_inc(p_exp_ready, 1)

            def step(b, par, r, prev=True, nxt=True):
                if nxt:
                    row_means(b + 1, 1 - par, r + par, range(0, HALF))
                if prev:
                    turned_evac(b - 1)
                if nxt:
                    row_means(b + 1, 1 - par, r + par, range(HALF, T))
                gate(b, par)
                hom_evac(b, par, 0)
                if nxt:
                    row_squares(b + 1)
                if prev:
                    second_norm(b - 1, 1 - par, r - 1 + par, range(T))
                elu_exp(b, par, 0)
                if prev:
                    prob_exp(b - 1)
                if nxt:
                    project_evac(b + 1, 1 - par, range(0, 4))
                else:
                    copy_rows(b - 1, 1 - par)
                    keep(b - 1, 1 - par)
                hom_evac(b, par, 1)
                if nxt:
                    project_evac(b + 1, 1 - par, range(4, 7))
                    elu_exp(b, par, 1)
                    project_evac(b + 1, 1 - par, range(7, T))
                if prev and nxt:
                    copy_rows(b - 1, 1 - par)
                    keep(b - 1, 1 - par)

            row_means(0, 0, 0, range(T))
            row_squares(0)
            project_evac(0, 0, range(T))
            step(0, 0, 0, prev=False)
            step(1, 1, 0)
            step(2, 0, 1)
            with act.Fori(1, B // 2 - 1) as i:
                step(2 * i + 1, 1, i)
                step(2 * i + 2, 0, i + 1)
            step(B - 1, 1, B // 2 - 1, nxt=False)

            def tile_step(i, c):
                tau = R * i + c
                known = isinstance(tau, int)
                t = tau + 2
                if not known or t < TILES:
                    act.wait_ge(rt_turned, t + 1)
                    act.activation(rt_t[:, c % 2, :], bank[4 + c % 2][:, 0:P], ACT.Copy).then_inc(rt_t_ready, 1)
                t = tau - 1
                if not known or t >= 0:
                    act.wait_ge(y_biased, t + 1)
                    act.activation(y_out[:, (c - 1) % R, :], y_b[:, (c + 1) % 2, :], ACT.Copy,
                                   scale=rt[:, (c - 1) % R, D + 1:D + 2]).then_inc(y_scaled, 1)
                t = tau + 1
                if not known or 0 <= t < TILES:
                    act.wait_ge(h_ready[0], t + 1)
                    for j in range(HC // 2):
                        m = act.activation(h_t[:, (c + 1) % 2, j * P:(j + 1) * P],
                                           bank[2 * ((c + 1) % 2)][:, j * P:(j + 1) * P], ACT.Relu,
                                           bias=w1[:, (c + 1) % R, H + j:H + j + 1])
                    m.then_inc(h_t_ready[0], 1)

            def store(b):
                act.wait_ge(out_ready, b + 1)
                act.dma_start(out[bass.ds(b, 1), :, :].rearrange("b p n -> (b p) n"), x1[:, cols(b * TD, TD)]
                              ).then_inc(stored, 16)

            def step_and_store(i, c):
                tile_step(i, c)
                if c == R // 2 and storing[0]:
                    store(i - (C_TURN + 1))

            storing = [False]

            def start_storing(i):
                storing[0] = True

            def beside(c):
                if c == 0:
                    elu_exp(B - 1, 1, 1)
                if c == 1:
                    act.wait_ge(x1_ready, 2 * B)
                    keep(B - 1, 1)
                if c == 2:
                    turned_evac(B - 1, bank[6:8])
                if c == 4:
                    prob_exp(B - 1)
                if 4 <= c < 8:
                    second_norm(B - 1, 1, B // 2 - 1, range(2 * c - 8, 2 * c - 6))
                if c == 8:
                    copy_rows(B - 1, 1)

            run_tiles(act, step_and_store, -2, beside, (C_TURN + 1,), start_storing)

            with act.Fori(B0 - 1, B - 1) as b:
                store(b)
            for h in range(2):
                half = slice(h * TD // 2, (h + 1) * TD // 2)
                act.wait_ge(out_ready, B + h)
                act.dma_start(out[B - 1, :, half], x1[:, (B - 1) * TD:B * TD][:, half]).then_inc(stored, 16)
            act.wait_ge(stored, 16 * (B + 1))

        @block.vector
        def _(dve):
            steps = [0]

            def fresh():
                dve.sem_clear(dve_chain)
                steps[0] = 0

            def link(ins):
                steps[0] += 1
                ins.then_inc(dve_chain, 1)
                dve.wait_ge(dve_chain, steps[0])

            def row_stats(b, par, tiles):
                fresh()
                if tiles[0] == 0:
                    dve.wait_ge(x1_ready, 2 * b + 1)
                    if not isinstance(b, int) or b >= 1:
                        dve.wait_ge(shift_ready, b)
                else:
                    dve.wait_ge(x1_ready, 2 * (b + 1))
                dve.sem_inc(dve_waits, 1)
                for t in tiles:
                    last = dve.bn_stats(stats[:, t, :], z_sb[:, par, t, :])
                link(last)
                for t in tiles:
                    last = dve.bn_aggr(mean_var[:, t, :], stats[:, t, :])
                if tiles[-1] == T - 1:
                    last.then_inc(stats_ready, 1)

            def column_sums(b, par, r, q):
                a = adj_sb[:, par, :].rearrange("p (c n) -> p c n", c=T)
                fresh()
                dve.wait_ge(adj_loaded[par][q], 16 * (r + 1))
                if q == 0:
                    if not isinstance(b, int) or b >= 1:
                        dve.wait_ge(deg_summed, b)
                    dve.tensor_tensor(col_sum[:, :], a[:, 0, :], a[:, 1, :], ALU.add).then_inc(sum_parts, 1)
                    return
                dve.wait_ge(sum_parts, QT * b + q)
                link(dve.tensor_tensor(col_sum[:, :], col_sum[:, :], a[:, 2 * q, :], ALU.add))
                dve.tensor_tensor(col_sum[:, :], col_sum[:, :], a[:, 2 * q + 1, :], ALU.add).then_inc(sum_parts, 1)

            def gate_bias(b, par):
                dve.wait_ge(proj_read, T * (b + 1))
                g = het_gate[:, par, :, D:2 * D]
                dve.tensor_tensor(g, g, b_gate_sb[:, :].rearrange("p (o d) -> p o d", o=1).broadcast_to((P, T, D)),
                                  ALU.add).then_inc(gate_biased, 1)

            def degree(b, ps=deg_ps):
                dve.wait_ge(deg_summed, b + 1)
                if not isinstance(b, int) or b >= 1:
                    dve.wait_ge(norm_ready, b)
                dve.tensor_scalar(deg_sb[:, :], ps, DEG_EPS, None, ALU.add).then_inc(deg_read, 1)

            def combine(b, par, h):
                sl = slice(h * HALF, (h + 1) * HALF)
                het = het_gate[:, par, sl, 0:D]
                th = het_gate[:, par, sl, D:2 * D]
                z = z_sb[:, par, sl, :]
                fresh()
                dve.wait_ge(hom_read, 2 * b + h + 1)
                link(dve.tensor_tensor(z, z, het, ALU.subtract))
                dve.wait_ge(gate_ready, b + 1)
                link(dve.scalar_tensor_tensor(z, th, 1.0, z, ALU.add, ALU.mult))
                dve.scalar_tensor_tensor(z, z, 0.5, het, ALU.mult, ALU.add).then_inc(z_ready, 1)

            def residual(b, par, h):
                sl = slice(h * HALF, (h + 1) * HALF)
                z = z_sb[:, par, sl, :]
                zf = z.rearrange("p t d -> p (t d)")
                fresh()
                dve.wait_ge(exp_ready, 2 * b + h + 1)
                link(dve.scalar_tensor_tensor(z, z, 0.0, neg_sb[:, sl, :], ALU.max, ALU.add))
                dve.scalar_tensor_tensor(zf, zf, -1.0, x1[:, cols(b * TD + h * HALF * D, HALF * D)], ALU.add, ALU.add
                                         ).then_inc(x1_ready, 1)

            def top_two(b, par):
                fresh()
                dve.wait_ge(gated, b + 1)
                dve.wait_ge(rstd_ready, b + 1)
                link(dve.tensor_tensor(scores[:, :, :], gate_ps.rearrange("p (t e) -> p t e", t=T),
                                       rstd[:, :].rearrange("p (t o) -> p t o", o=1).broadcast_to((P, T, NE)),
                                       ALU.mult))
                dve.tensor_tensor(scores[:, :, :], scores[:, :, :],
                                  b_router_sb[:, :].rearrange("p (o e) -> p o e", o=1).broadcast_to((P, T, NE)),
                                  ALU.add).then_inc(scores_ready, 1)
                dve.wait_ge(pool_const, 1)
                dve.wait_ge(scores_ready, b + 1)
                for t in range(T):
                    last = dve.max(top[:, t, :], scores[:, t, :])
                link(last)
                dve.tensor_tensor(p_exp[:, :], top[:, :, 1], top[:, :, 0], ALU.subtract).then_inc(gaps_ready, 1)
                for t in range(T):
                    last = dve.max_index(top_at[:, t, :], top[:, t, :], scores[:, t, :])
                link(last)

            def choose(b, par, r):
                link(dve.tensor_copy(top_f[:, :, :], top_at[:, :, 0:K].rearrange("p t k -> p k t")))
                iota4 = iota_e[:, :].rearrange("p (k t e) -> p k t e", k=1, t=1).broadcast_to((P, K, T, NE))
                top4 = top_f[:, :, :].rearrange("p k (t o) -> p k t o", o=1).broadcast_to((P, K, T, NE))
                link(dve.tensor_tensor(chosen[:, :, :, :], iota4, top4, ALU.is_equal))
                dve.tensor_tensor(picked[:, :, :], chosen[:, 0, :, :], chosen[:, 1, :, :], ALU.add
                                  ).then_inc(picked_ready, 1)
                if not isinstance(b, int) or b >= 2:
                    dve.wait_ge(scattered[par], 16 * K * T * r)
                to = payload[:, par, :, :, D:D + 1].bitcast(I32)
                dve.tensor_scalar(to, to, float(2 * N), None, ALU.add)
                dve.wait_ge(p_exp_ready, b + 1)
                link(dve.tensor_scalar(p_sum[:, :], p_exp[:, :], 1.0, None, ALU.add))
                prob = [payload[:, par, k, :, D + 1] for k in range(K)]
                link(dve.reciprocal(prob[0], p_sum[:, :]))
                dve.tensor_tensor(prob[1], p_exp[:, :], prob[0], ALU.mult)

            def place_rows(b, par):
                fresh()
                dve.wait_ge(ranked, b + 1)
                now = next_row[:, cols(b * NE, NE)]
                nr = now.rearrange("p (o e) -> p o e", o=1).broadcast_to((P, T, NE))
                link(dve.tensor_tensor(place[:, :, :], rank_ps.rearrange("p (t e) -> p t e", t=T), nr, ALU.add))
                dve.tensor_tensor(next_row[:, cols((b + 1) * NE, NE)], now, total_ps, ALU.add)
                pl = place[:, :, :].rearrange("p (o t) e -> p o t e", o=1).broadcast_to((P, K, T, NE))
                link(dve.tensor_tensor(place_k[:, :, :, :], chosen[:, :, :, :], pl, ALU.mult))
                link(dve.tensor_reduce(slot_f[:, :, :], place_k[:, :, :, :], AX_X, ALU.add))
                dve.tensor_scalar(slot[:, par, :, :], slot_f[:, :, :], group_at[:, cols(b, 1)], None, ALU.add
                                  ).then_inc(slots_ready, 1)

            def tile_table(g, parts):
                first, end = [next_row[:, b * NE:(b + 1) * NE] for b in first_batch[g:g + 2]]
                at = group_at[:, first_batch[g]:first_batch[g] + 1]
                iota, reaches = tile_iota[:, 0:GT[g]], reach[:, 0:GT[g], :]
                wide = (P, GT[g], NE)
                mine = slice(first_tile[g], first_tile[g + 1])
                fresh()
                if 0 in parts:
                    dve.wait_ge(slots_ready, first_batch[g + 1])
                    dve.tensor_scalar(pad_at[:, g, :], end, at, None, ALU.add).then_inc(pad_at_ready, 1)
                    link(dve.tensor_tensor(tiles_e[:, :], end, first, ALU.subtract))
                    link(dve.tensor_scalar(count_i[:, :], tiles_e[:, :], float(P - 1), None, ALU.add))
                    link(dve.tensor_scalar(count_i[:, :], count_i[:, :], 7, None, ALU.logical_shift_right))
                    link(dve.tensor_copy(tiles_e[:, :], count_i[:, :]))
                if 1 in parts:
                    link(dve.tensor_tensor(tiles_upto[:, :, :], upto[:, :, :],
                                           tiles_e[:, :].rearrange("p (o f) -> p o f", o=1).broadcast_to((P, NE, NE)),
                                           ALU.mult))
                    link(dve.tensor_reduce(tiles_end[:, :], tiles_upto[:, :, :], AX_X, ALU.add))
                if 2 in parts:
                    link(dve.tensor_tensor(tiles_e[:, :], tiles_e[:, :], tiles_end[:, :], ALU.subtract))
                    link(dve.scalar_tensor_tensor(row_of[:, 0:NE], tiles_e[:, :], float(P), first, ALU.mult, ALU.add))
                    dve.tensor_scalar(row_of[:, NE:NE + 1], tiles_end[:, NE - 1:NE], -float(P), float(G * GROWS),
                                      ALU.mult, ALU.add)
                    link(dve.tensor_scalar(row_of[:, 0:NE], row_of[:, 0:NE], at, None, ALU.add))
                    link(dve.tensor_tensor(row_step[:, :], row_of[:, 1:NE + 1], row_of[:, 0:NE], ALU.subtract))
                if 3 in parts:
                    link(dve.tensor_tensor(reaches, iota.rearrange("p (t o) -> p t o", o=1).broadcast_to(wide),
                                           tiles_end[:, :].rearrange("p (o e) -> p o e", o=1).broadcast_to(wide),
                                           ALU.is_ge))
                if 4 in parts:
                    link(dve.tensor_reduce(tile_e[:, 0:GT[g]], reaches, AX_X, ALU.add))
                if 5 in parts:
                    link(dve.tensor_tensor(reaches, reaches,
                                           row_step[:, :].rearrange("p (o e) -> p o e", o=1).broadcast_to(wide),
                                           ALU.mult))
                if 6 in parts:
                    link(dve.tensor_reduce(tile_row[:, 0:GT[g]], reaches, AX_X, ALU.add))
                if 7 in parts:
                    link(dve.scalar_tensor_tensor(tile_row[:, 0:GT[g]], iota, float(P), tile_row[:, 0:GT[g]],
                                                  ALU.mult, ALU.add))
                    dve.tensor_scalar(tab_w2[:, mine], tile_e[:, 0:GT[g]], float(NE - 1), float(H), ALU.min, ALU.mult)
                    dve.tensor_scalar(tab_e[:, mine], tile_e[:, 0:GT[g]], float(NE - 1), float(P), ALU.min, ALU.mult)
                    dve.tensor_scalar(tab_row[:, mine], tile_row[:, 0:GT[g]], row_of[:, 0:1], None, ALU.add
                                      ).then_inc(tables_ready, 1)

            def sums(b, par, r, parts):
                if not isinstance(b, int) or b < B:
                    for q in parts:
                        column_sums(b, par, r, q)

            def step(b, par, r, prev=True, nxt=True, nxt2=True):
                if prev:
                    row_stats(b - 1, 1 - par, range(HALF, T))
                gate_bias(b, par)
                if nxt:
                    sums(b + 1, 1 - par, r + par, range(2, QT))
                else:
                    tile_table(0, range(6, 8))
                combine(b, par, 0)
                if nxt:
                    degree(b + 1)
                if prev:
                    top_two(b - 1, 1 - par)
                    choose(b - 1, 1 - par, r - 1 + par)
                residual(b, par, 0)
                if nxt:
                    if prev:
                        place_rows(b - 1, 1 - par)
                    row_stats(b, par, range(0, HALF))
                if nxt2:
                    sums(b + 2, par, r + 1, range(0, 1))
                elif nxt:
                    tile_table(0, range(0, 4))
                combine(b, par, 1)
                if nxt2:
                    sums(b + 2, par, r + 1, range(1, 2))
                elif nxt:
                    tile_table(0, range(4, 6))
                if nxt:
                    residual(b, par, 1)

            dve.wait_ge(pool_const, 1)
            dve.wait_ge(s_const, 48)
            dve.wait_ge(w_summed, 1)
            dve.scalar_tensor_tensor(w_centred_sb[:, :], w_sum_ps, -1.0 / D, w_raw[:, :], ALU.mult, ALU.add
                                     ).then_inc(w_centred, 1)
            sums(0, 0, 0, range(QT))
            degree(0, deg_0_ps)
            dve.wait_ge(proj_read, T)
            dve.wait_ge(norm_ready, 1)
            for h in range(2):
                sl = slice(h * HALF, (h + 1) * HALF)
                dve.tensor_tensor(f_hom[:, sl, :], f_hom[:, sl, :], norm_rstd[:, 0, 0, sl].rearrange(
                    "p (t o) -> p t o", o=1).broadcast_to((P, HALF, D)), ALU.mult).then_inc(f_hom_ready, 1)
            sums(1, 1, 0, range(0, 2))
            step(0, 0, 0, prev=False)
            step(1, 1, 0)
            step(2, 0, 1)
            with dve.Fori(1, B // 2 - 2) as i:
                step(2 * i + 1, 1, i)
                step(2 * i + 2, 0, i + 1)
            step(B - 3, 1, B // 2 - 2)
            step(B - 2, 0, B // 2 - 1, nxt2=False)
            step(B - 1, 1, B // 2 - 1, nxt=False, nxt2=False)

            def result_step(i, c):
                tau = R * i + c
                known = isinstance(tau, int)
                t = tau - 1
                if not known or t >= 0:
                    s = (c - 1) % R
                    if not known or t >= R:
                        dve.wait_ge(returned[s], 16 * (i + (c - 1) // R))
                    dve.tensor_copy(dest[:, s:s + 1], rt[:, s, D:D + 1].bitcast(I32))
                    if known and t == 0:
                        dve.wait_ge(s_bias, 16)
                    col = dve.value_load(tab_e[0:1, cols(t, 1)], min_val=0, max_val=(NE - 1) * D)
                    dve.wait_ge(y_ready, t + 1)
                    if not known or t >= 2:
                        dve.wait_ge(y_scaled, t - 1)
                    dve.tensor_tensor(y_b[:, (c + 1) % 2, :], bank[6 + (c + 1) % 2][:, 0:D],
                                      b2_sb[:, cols(col, D)], ALU.add).then_inc(y_biased, 1)

            def hidden_step(i, c):
                tau = R * i + c
                known = isinstance(tau, int)
                t = tau + 1
                if not known or 0 <= t < TILES:
                    dve.wait_ge(h_ready[1], t + 1)
                    for j in range(HC // 2):
                        n = HC // 2 + j
                        m = dve.tensor_scalar(h_t[:, (c + 1) % 2, n * P:(n + 1) * P],
                                              bank[1 + 2 * ((c + 1) % 2)][:, j * P:(j + 1) * P],
                                              w1[:, (c + 1) % R, H + n:H + n + 1], 0.0, ALU.add, ALU.max)
                    m.then_inc(h_t_ready[1], 1)

            def tile_step(i, c):
                result_step(i, c)
                hidden_step(i, c)

            def add_choices(b, par, r, part, parts):
                at = slice(part * TD // parts, (part + 1) * TD // parts)
                fresh()
                dve.wait_ge(y_loaded[par], 16 * K * (r + 1))
                link(dve.tensor_tensor(y_in[:, par, 0, at], y_in[:, par, 0, at], y_in[:, par, 1, at], ALU.add))

            def add_residual(b, par, part, parts):
                n = TD // parts
                xb = x1[:, cols(b * TD + part * n, n)]
                last = dve.tensor_tensor(xb, xb, y_in[:, par, 0, part * n:(part + 1) * n], ALU.add)
                if part == parts - 1:
                    last.then_inc(out_ready, 1)

            def beside(c):
                if c == 0:
                    residual(B - 1, 1, 1)
                if c == 2:
                    row_stats(B - 1, 1, range(0, HALF))
                    row_stats(B - 1, 1, range(HALF, T))
                if c == 3:
                    top_two(B - 1, 1)
                if c == 4:
                    choose(B - 1, 1, B // 2 - 1)
                if c == 6:
                    place_rows(B - 1, 1)

            tile_step(-1, R - 1)
            place_rows(B - 2, 0)
            for c in range(R + 1):
                tile_step(0, c)
                beside(c)
            for c in range(1, R + 1):
                result_step(1, c)
                tile_table(1, range(c - 1, c))
                hidden_step(1, c)
            with dve.Fori(2, C_TURN) as i:
                for c in range(1, R + 1):
                    tile_step(i, c)
            with dve.Fori(0, B0 // 2) as r:
                for par in range(2):
                    for c in range(1, R + 1):
                        result_step(C_TURN + 2 * r + par, c)
                        add_choices(2 * r + par, par, r, c - 1, R)
                        hidden_step(C_TURN + 2 * r + par, c)
                        add_residual(2 * r + par, par, c - 1, R)
            for c in range(1, R + 1):
                result_step(TURNS - 1, c)
                add_choices(B0 - 1, 0, B0 // 2, c - 1, R)
                hidden_step(TURNS - 1, c)
                add_residual(B0 - 1, 0, c - 1, R)
            for b in range(B0, B - 1):
                add_choices(b, b % 2, b // 2, 0, 1)
                add_residual(b, b % 2, 0, 1)
            for h in range(2):
                at = slice(h * TD // 2, (h + 1) * TD // 2)
                xb = x1[:, (B - 1) * TD:B * TD][:, at]
                fresh()
                dve.wait_ge(y_last_loaded[h], 16 * K)
                link(dve.tensor_tensor(y_in[:, 2, 0, at], y_in[:, 2, 0, at], y_in[:, 2, 1, at], ALU.add))
                dve.tensor_tensor(xb, xb, y_in[:, 2, 0, at], ALU.add).then_inc(out_ready, 1)


def kernel(x, adj, L0_gnn_W_t, L0_gnn_b_t, L0_gnn_W_h, L0_gnn_theta, L0_ffn_Wg, L0_ffn_bg, L0_ffn_W1, L0_ffn_b1,
           L0_ffn_W2, L0_ffn_b2):
    import numpy as np
    import concourse.bacc as bacc
    from concourse.bass_utils import run_bass_kernel_spmd as launch

    b, n, d = x.shape
    t = n // P
    ne, h, _ = L0_ffn_W1.shape
    c = np.ascontiguousarray
    rows = lambda a: c(np.broadcast_to(np.asarray(a).reshape(1, -1), (P, a.size)))
    adj_t = np.asarray(adj).reshape(b, P, t, P, t).transpose(0, 3, 4, 2, 1)
    w1_t = np.asarray(L0_ffn_W1).transpose(0, 2, 1)
    b1_t = np.asarray(L0_ffn_b1).reshape(ne, h // P, P).transpose(0, 2, 1)
    w2_t = np.asarray(L0_ffn_W2).reshape(ne, d, h // P, P).transpose(3, 0, 2, 1)
    arrays = {
        "x": c(np.asarray(x).reshape(b, P, t * d)),
        "x_t": c(np.asarray(x).reshape(b, P, t, d).transpose(0, 3, 2, 1)).reshape(b, d, n),
        "adj_t": c(adj_t).reshape(b, P, t * n),
        "weights": c(np.concatenate([np.asarray(a) for a in (L0_gnn_theta, L0_gnn_W_h, L0_gnn_W_t)]
                                    + [np.asarray(L0_ffn_Wg).T], 1)),
        "b_gate": rows(np.asarray(L0_gnn_b_t)),
        "b_router": rows(np.asarray(L0_ffn_bg)),
        "w1b_t": c(np.concatenate([w1_t, b1_t], 2)).reshape(ne * d, h + h // P),
        "w2_t": c(w2_t).reshape(P, ne * h),
        "b2": rows(np.asarray(L0_ffn_b2)),
    }
    nc = bacc.Bacc("TRN2", target_bir_lowering=False, num_devices=1)
    args = [nc.dram_tensor(f"in_{k}", a.shape, F32, kind="ExternalInput").ap() for k, a in arrays.items()]
    out = nc.dram_tensor("out", (b, P, t * d), F32, kind="ExternalOutput").ap()
    build(nc, *args, out)
    got = launch(nc, [{f"in_{k}": a for k, a in arrays.items()}], core_ids=[0])
    return got.results[0]["out"].reshape(b, n, d)
```
